# Optimizing a Trainium2 kernel written in Bass

```python
import numpy as np
import jax
import jax.numpy as jnp

def _softmax(x, axis=-1):
    return jax.nn.softmax(x, axis=axis)

def _gelu(x):
    return jax.nn.gelu(x, approximate=True)

def _silu(x):
    return jax.nn.silu(x)

def _sigmoid(x):
    return jax.nn.sigmoid(x)

def _layernorm(x, axis=-1, eps=1e-05):
    m = jnp.mean(x, axis=axis, keepdims=True)
    v = jnp.var(x, axis=axis, keepdims=True)
    return (x - m) / jnp.sqrt(v + eps)

def _scatter_add(tgt, idx, src, axis=0):
    return tgt.at[idx].add(src)

def _segment_sum(src, seg, n):
    return jax.ops.segment_sum(src, seg, n)
kernel_name = 'mk_decoder_preln_d1_seqx_r4_d31f13'

def setup_inputs(seed: int=0):
    np.random.seed(seed)
    _w = jnp.asarray

    def _rec_inputs():
        import jax
        import jax.numpy as jnp
        _rk = jax.random.key(seed)
        x = 7.22e-05 + 1 * jax.random.normal(jax.random.fold_in(_rk, 1), (4, 512, 256), jnp.float32)
        _lenS = 512 - jax.random.randint(jax.random.fold_in(_rk, 7), (4,), 0, max(1, 512 // 4) + 1, jnp.int32)
        _lenS2 = 1024 - jax.random.randint(jax.random.fold_in(_rk, 8), (4,), 0, max(1, 1024 // 4) + 1, jnp.int32)
        _ctx_1024P = jax.random.normal(jax.random.fold_in(_rk, 11), (4, 16, 256), jnp.float32)
        _ctx_1024c = jax.random.dirichlet(jax.random.fold_in(_rk, 511), 0.3 * jnp.ones((16,), jnp.float32), (4, 1024))
        _ctx_1024t = jnp.einsum('bsk,bkd->bsd', _ctx_1024c, _ctx_1024P)
        _ctx_1024t = _ctx_1024t * jax.lax.rsqrt(jnp.mean(jnp.square(_ctx_1024t)) + 1e-12) * 0.953939
        ctx_1024 = 4.13588e-05 + 0.999923 * (_ctx_1024t + 0.3 * jax.random.normal(jax.random.fold_in(_rk, 611), (4, 1024, 256), jnp.float32))
        return (x, ctx_1024)
    x, ctx_1024 = _rec_inputs()

    def _L0_attn_setup():
        import jax, jax.numpy as jnp
        import numpy as np
        import math
        NUM_HEADS = 8
        EMB = 256
        HEAD_DIM = 128
        B, T = (1, 1024)

        def sinusoidal_pe(T, d, dtype=jnp.float32):
            pos = jnp.arange(T, dtype=dtype)[:, None]
            inv_freq = jnp.exp(-math.log(10000.0) * jnp.arange(0, d, 2, dtype=dtype) / d)
            ang = pos * inv_freq[None, :]
            pe = jnp.zeros((T, d), dtype=dtype)
            pe = pe.at[:, 0::2].set(jnp.sin(ang))
            pe = pe.at[:, 1::2].set(jnp.cos(ang))
            return pe
        key = jax.random.key(seed)
        ks = jax.random.split(key, 6)
        s = lambda fan_in: 1.0 / math.sqrt(fan_in)
        x = jax.random.normal(ks[0], (B, T, EMB), dtype=jnp.float32)
        Wq = jax.random.normal(ks[1], (EMB, NUM_HEADS * HEAD_DIM), dtype=jnp.float32) * s(EMB)
        bq = jax.random.normal(ks[2], (NUM_HEADS * HEAD_DIM,), dtype=jnp.float32) * s(EMB)
        Wkv = jax.random.normal(ks[3], (EMB, 2 * HEAD_DIM), dtype=jnp.float32) * s(EMB)
        bkv = jax.random.normal(ks[4], (2 * HEAD_DIM,), dtype=jnp.float32) * s(EMB)
        Wo = jax.random.normal(ks[5], (NUM_HEADS * HEAD_DIM, EMB), dtype=jnp.float32) * s(NUM_HEADS * HEAD_DIM)
        return {'x': x, 'Wq': Wq, 'bq': bq, 'Wkv': Wkv, 'bkv': bkv, 'Wo': Wo}
    _L0_attn_all = _L0_attn_setup()
    _L0_attn_in = {k: v for k, v in _L0_attn_all.items() if k in ('Wq', 'bq', 'Wkv', 'bkv', 'Wo')}
    del _L0_attn_all

    def _L0_xattn_setup():
        import jax, jax.numpy as jnp
        import numpy as np
        B, L, D_MODEL, H = (4, 512, 256, 16)
        E = D_MODEL // H
        EPS = 1e-05

        def layernorm(x, w, b):
            mu = jnp.mean(x, axis=-1, keepdims=True)
            var = jnp.mean((x - mu) ** 2, axis=-1, keepdims=True)
            return (x - mu) * jax.lax.rsqrt(var + EPS) * w + b
        key = jax.random.key(seed)
        ks = jax.random.split(key, 12)
        s_in = 1.0 / np.sqrt(D_MODEL)
        inp = {'q': jax.random.normal(ks[0], (B, L, D_MODEL), jnp.float32), 'k': jax.random.normal(ks[1], (B, L, D_MODEL), jnp.float32), 'v': jax.random.normal(ks[2], (B, L, D_MODEL), jnp.float32), 'norm_w': jnp.ones((D_MODEL,), jnp.float32), 'norm_b': jnp.zeros((D_MODEL,), jnp.float32), 'norm1_w': jnp.ones((D_MODEL,), jnp.float32), 'norm1_b': jnp.zeros((D_MODEL,), jnp.float32), 'Wq': jax.random.uniform(ks[3], (D_MODEL, H * E), jnp.float32, -s_in, s_in), 'bq': jnp.zeros((H * E,), jnp.float32), 'Wk': jax.random.uniform(ks[4], (D_MODEL, H * E), jnp.float32, -s_in, s_in), 'bk': jnp.zeros((H * E,), jnp.float32), 'Wv': jax.random.uniform(ks[5], (D_MODEL, H * E), jnp.float32, -s_in, s_in), 'bv': jnp.zeros((H * E,), jnp.float32), 'Wo': jax.random.uniform(ks[6], (H * E, D_MODEL), jnp.float32, -s_in, s_in), 'bo': jnp.zeros((D_MODEL,), jnp.float32)}
        return inp
    _L0_xattn_all = _L0_xattn_setup()
    _L0_xattn_in = {k: v for k, v in _L0_xattn_all.items() if k in ('norm_w', 'norm_b', 'norm1_w', 'norm1_b', 'Wq', 'bq', 'Wk', 'bk', 'Wv', 'bv', 'Wo', 'bo')}
    del _L0_xattn_all

    def _L0_ffn_setup():
        import jax, jax.numpy as jnp
        import numpy as np
        N_GROUP = 8
        TOPK_GROUP = 4
        TOPK = 8
        ROUTED_SCALE = 2.5
        B, S, D, F, E = (4, 512, 256, 128, 64)

        def _route(x, w_router, b_router):
            scores = jax.nn.sigmoid(jnp.einsum('bsd,de->bse', x, w_router)).astype(jnp.float32)
            swb = scores + b_router
            e = scores.shape[-1]
            group_scores = jnp.sum(jax.lax.top_k(swb.reshape(swb.shape[:-1] + (N_GROUP, -1)), 2)[0], axis=-1)
            group_idx = jax.lax.top_k(group_scores, TOPK_GROUP)[1]
            mask = jnp.any(jnp.arange(N_GROUP)[:, None] == group_idx[..., None, :], axis=-1)
            mask = jnp.repeat(mask, e // N_GROUP, axis=-1)
            masked_scores = jnp.where(mask, swb, 0.0)
            topk_idx = jax.lax.top_k(masked_scores, TOPK)[1]
            topk_w = jnp.take_along_axis(scores, topk_idx, axis=-1).astype(jnp.float32)
            topk_w = ROUTED_SCALE * topk_w / (jnp.sum(topk_w, axis=-1)[..., None] + 1e-20)
            return (topk_w, topk_idx)

        def _moe_forward(x, w_router, b_router, we_gate, we_up, we_down, ws_gate, ws_up, ws_down):
            b, s, d = x.shape
            e = we_gate.shape[0]
            topk_w, topk_idx = _route(x, w_router, b_router)
            x_flat = x.reshape(-1, d)
            idx_flat = topk_idx.reshape(-1)
            sort = jnp.argsort(idx_flat)
            tok = sort // TOPK
            x_sorted = x_flat[tok]
            group_sizes = jnp.bincount(idx_flat, length=e).astype(jnp.int32)
            g = jax.lax.ragged_dot(x_sorted, we_gate, group_sizes)
            u = jax.lax.ragged_dot(x_sorted, we_up, group_sizes)
            o = jax.lax.ragged_dot(jax.nn.silu(g) * u, we_down, group_sizes)
            w_sorted = topk_w.reshape(-1)[sort].astype(o.dtype)
            y = jnp.zeros_like(x_flat).at[tok].add(o * w_sorted[:, None])
            y = y.reshape(b, s, d)
            shared = jnp.einsum('btf,fd->btd', jax.nn.silu(jnp.einsum('btd,df->btf', x, ws_gate)) * jnp.einsum('btd,df->btf', x, ws_up), ws_down)
            return y + shared
        key = jax.random.key(seed)
        ks = jax.random.split(key, 10)
        sd = 1.0 / np.sqrt(D)
        sf = 1.0 / np.sqrt(F)
        return {'x': jax.random.normal(ks[0], (B, S, D), jnp.float32), 'w_router': jax.random.normal(ks[1], (D, E), jnp.float32) * sd, 'b_router': jax.random.normal(ks[2], (E,), jnp.float32) * 0.1, 'we_gate': jax.random.normal(ks[3], (E, D, F), jnp.float32) * sd, 'we_up': jax.random.normal(ks[4], (E, D, F), jnp.float32) * sd, 'we_down': jax.random.normal(ks[5], (E, F, D), jnp.float32) * sf, 'ws_gate': jax.random.normal(ks[6], (D, F), jnp.float32) * sd, 'ws_up': jax.random.normal(ks[7], (D, F), jnp.float32) * sd, 'ws_down': jax.random.normal(ks[8], (F, D), jnp.float32) * sf}
    _L0_ffn_all = _L0_ffn_setup()
    _L0_ffn_in = {k: v for k, v in _L0_ffn_all.items() if k in ('w_router', 'b_router', 'we_gate', 'we_up', 'we_down', 'ws_gate', 'ws_up', 'ws_down')}
    del _L0_ffn_all
    return {'x': x, 'ctx_1024': ctx_1024, 'L0_attn_Wq': _L0_attn_in['Wq'], 'L0_attn_bq': _L0_attn_in['bq'], 'L0_attn_Wkv': _L0_attn_in['Wkv'], 'L0_attn_bkv': _L0_attn_in['bkv'], 'L0_attn_Wo': _L0_attn_in['Wo'], 'L0_xattn_norm_w': _L0_xattn_in['norm_w'], 'L0_xattn_norm_b': _L0_xattn_in['norm_b'], 'L0_xattn_norm1_w': _L0_xattn_in['norm1_w'], 'L0_xattn_norm1_b': _L0_xattn_in['norm1_b'], 'L0_xattn_Wq': _L0_xattn_in['Wq'], 'L0_xattn_bq': _L0_xattn_in['bq'], 'L0_xattn_Wk': _L0_xattn_in['Wk'], 'L0_xattn_bk': _L0_xattn_in['bk'], 'L0_xattn_Wv': _L0_xattn_in['Wv'], 'L0_xattn_bv': _L0_xattn_in['bv'], 'L0_xattn_Wo': _L0_xattn_in['Wo'], 'L0_xattn_bo': _L0_xattn_in['bo'], 'L0_ffn_w_router': _L0_ffn_in['w_router'], 'L0_ffn_b_router': _L0_ffn_in['b_router'], 'L0_ffn_we_gate': _L0_ffn_in['we_gate'], 'L0_ffn_we_up': _L0_ffn_in['we_up'], 'L0_ffn_we_down': _L0_ffn_in['we_down'], 'L0_ffn_ws_gate': _L0_ffn_in['ws_gate'], 'L0_ffn_ws_up': _L0_ffn_in['ws_up'], 'L0_ffn_ws_down': _L0_ffn_in['ws_down']}

def reference(x, ctx_1024, L0_attn_Wq, L0_attn_bq, L0_attn_Wkv, L0_attn_bkv, L0_attn_Wo, L0_xattn_norm_w, L0_xattn_norm_b, L0_xattn_norm1_w, L0_xattn_norm1_b, L0_xattn_Wq, L0_xattn_bq, L0_xattn_Wk, L0_xattn_bk, L0_xattn_Wv, L0_xattn_bv, L0_xattn_Wo, L0_xattn_bo, L0_ffn_w_router, L0_ffn_b_router, L0_ffn_we_gate, L0_ffn_we_up, L0_ffn_we_down, L0_ffn_ws_gate, L0_ffn_ws_up, L0_ffn_ws_down):
    import jax
    import jax.numpy as jnp

    def _L0_attn_ref(x, Wq, bq, Wkv, bkv, Wo):
        import jax, jax.numpy as jnp
        import numpy as np
        import math
        NUM_HEADS = 8
        EMB = 256
        HEAD_DIM = 128
        B, T = (1, 1024)

        def sinusoidal_pe(T, d, dtype=jnp.float32):
            pos = jnp.arange(T, dtype=dtype)[:, None]
            inv_freq = jnp.exp(-math.log(10000.0) * jnp.arange(0, d, 2, dtype=dtype) / d)
            ang = pos * inv_freq[None, :]
            pe = jnp.zeros((T, d), dtype=dtype)
            pe = pe.at[:, 0::2].set(jnp.sin(ang))
            pe = pe.at[:, 1::2].set(jnp.cos(ang))
            return pe
        Bsz, Tlen, E = x.shape
        q = (x @ Wq + bq).reshape(Bsz, Tlen, NUM_HEADS, HEAD_DIM)
        kv = x @ Wkv + bkv
        k, v = (kv[..., :HEAD_DIM], kv[..., HEAD_DIM:])
        q = jnp.transpose(q, (0, 2, 1, 3))
        pe = sinusoidal_pe(Tlen, HEAD_DIM, x.dtype)
        q = q + pe[None, None, :, :]
        k = k + pe[None, :, :]
        scale = 1.0 / math.sqrt(HEAD_DIM)
        scores = jnp.einsum('bhqd,bkd->bhqk', q, k) * scale
        causal = jnp.tril(jnp.ones((Tlen, Tlen), dtype=bool))
        scores = jnp.where(causal[None, None, :, :], scores, jnp.finfo(scores.dtype).min)
        probs = jax.nn.softmax(scores, axis=-1)
        attn = jnp.einsum('bhqk,bkd->bhqd', probs, v)
        out = jnp.transpose(attn, (0, 2, 1, 3)).reshape(Bsz, Tlen, NUM_HEADS * HEAD_DIM)
        return out @ Wo

    def _L0_xattn_ref(q, k, v, norm_w, norm_b, norm1_w, norm1_b, Wq, bq, Wk, bk, Wv, bv, Wo, bo):
        import jax, jax.numpy as jnp
        import numpy as np
        B, L, D_MODEL, H = (4, 512, 256, 16)
        E = D_MODEL // H
        EPS = 1e-05

        def layernorm(x, w, b):
            mu = jnp.mean(x, axis=-1, keepdims=True)
            var = jnp.mean((x - mu) ** 2, axis=-1, keepdims=True)
            return (x - mu) * jax.lax.rsqrt(var + EPS) * w + b
        b, l, _ = q.shape
        s = k.shape[1]
        qn = layernorm(q, norm_w, norm_b)
        kn = layernorm(k, norm_w, norm_b)
        vn = layernorm(v, norm_w, norm_b)
        Q = (qn @ Wq + bq).reshape(b, l, H, E)
        K = (kn @ Wk + bk).reshape(b, s, H, E)
        V = (vn @ Wv + bv).reshape(b, s, H, E)
        scale = 1.0 / jnp.sqrt(jnp.asarray(E, Q.dtype))
        scores = jnp.einsum('blhe,bshe->bhls', Q, K)
        A = jax.nn.softmax(scale * scores, axis=-1)
        O = jnp.einsum('bhls,bshd->blhd', A, V)
        O = O + Q
        out = jnp.transpose(O, (0, 2, 1, 3)).reshape(b, l, H * E)
        return layernorm(out, norm1_w, norm1_b) @ Wo + bo + out

    def _L0_ffn_ref(x, w_router, b_router, we_gate, we_up, we_down, ws_gate, ws_up, ws_down):
        import jax, jax.numpy as jnp
        import numpy as np
        N_GROUP = 8
        TOPK_GROUP = 4
        TOPK = 8
        ROUTED_SCALE = 2.5
        B, S, D, F, E = (4, 512, 256, 128, 64)

        def _route(x, w_router, b_router):
            scores = jax.nn.sigmoid(jnp.einsum('bsd,de->bse', x, w_router)).astype(jnp.float32)
            swb = scores + b_router
            e = scores.shape[-1]
            group_scores = jnp.sum(jax.lax.top_k(swb.reshape(swb.shape[:-1] + (N_GROUP, -1)), 2)[0], axis=-1)
            group_idx = jax.lax.top_k(group_scores, TOPK_GROUP)[1]
            mask = jnp.any(jnp.arange(N_GROUP)[:, None] == group_idx[..., None, :], axis=-1)
            mask = jnp.repeat(mask, e // N_GROUP, axis=-1)
            masked_scores = jnp.where(mask, swb, 0.0)
            topk_idx = jax.lax.top_k(masked_scores, TOPK)[1]
            topk_w = jnp.take_along_axis(scores, topk_idx, axis=-1).astype(jnp.float32)
            topk_w = ROUTED_SCALE * topk_w / (jnp.sum(topk_w, axis=-1)[..., None] + 1e-20)
            return (topk_w, topk_idx)

        def _moe_forward(x, w_router, b_router, we_gate, we_up, we_down, ws_gate, ws_up, ws_down):
            b, s, d = x.shape
            e = we_gate.shape[0]
            topk_w, topk_idx = _route(x, w_router, b_router)
            x_flat = x.reshape(-1, d)
            idx_flat = topk_idx.reshape(-1)
            sort = jnp.argsort(idx_flat)
            tok = sort // TOPK
            x_sorted = x_flat[tok]
            group_sizes = jnp.bincount(idx_flat, length=e).astype(jnp.int32)
            g = jax.lax.ragged_dot(x_sorted, we_gate, group_sizes)
            u = jax.lax.ragged_dot(x_sorted, we_up, group_sizes)
            o = jax.lax.ragged_dot(jax.nn.silu(g) * u, we_down, group_sizes)
            w_sorted = topk_w.reshape(-1)[sort].astype(o.dtype)
            y = jnp.zeros_like(x_flat).at[tok].add(o * w_sorted[:, None])
            y = y.reshape(b, s, d)
            shared = jnp.einsum('btf,fd->btd', jax.nn.silu(jnp.einsum('btd,df->btf', x, ws_gate)) * jnp.einsum('btd,df->btf', x, ws_up), ws_down)
            return y + shared
        return _moe_forward(x, w_router, b_router, we_gate, we_up, we_down, ws_gate, ws_up, ws_down)
    x = x + _L0_attn_ref(_layernorm(x, axis=-1), L0_attn_Wq, L0_attn_bq, L0_attn_Wkv, L0_attn_bkv, L0_attn_Wo)
    x = x + _L0_xattn_ref(_layernorm(x, axis=-1), ctx_1024, ctx_1024, L0_xattn_norm_w, L0_xattn_norm_b, L0_xattn_norm1_w, L0_xattn_norm1_b, L0_xattn_Wq, L0_xattn_bq, L0_xattn_Wk, L0_xattn_bk, L0_xattn_Wv, L0_xattn_bv, L0_xattn_Wo, L0_xattn_bo)
    x = x + _L0_ffn_ref(_layernorm(x, axis=-1), L0_ffn_w_router, L0_ffn_b_router, L0_ffn_we_gate, L0_ffn_we_up, L0_ffn_we_down, L0_ffn_ws_gate, L0_ffn_ws_up, L0_ffn_ws_down)
    return x

_drawn_inputs = setup_inputs


def setup_inputs(seed=0):
    import zlib

    import numpy as np

    out = dict(_drawn_inputs(seed))
    spreads = {'L0_xattn_norm_w': (1.0, 0.2),
     'L0_xattn_norm_b': (0.0, 0.1),
     'L0_xattn_norm1_w': (1.0, 0.2),
     'L0_xattn_norm1_b': (0.0, 0.1),
     'L0_xattn_bq': (0.0, 0.1),
     'L0_xattn_bk': (0.0, 0.1),
     'L0_xattn_bv': (0.0, 0.1),
     'L0_xattn_bo': (0.0, 0.1)}
    factors = {}
    for name, (base, spread) in spreads.items():
        noise = np.random.default_rng([zlib.crc32(name.encode()), seed]).standard_normal(out[name].shape)
        drawn = base * np.exp(spread * noise) if base else spread * noise
        out[name] = jnp.asarray(drawn.astype(out[name].dtype))
    for name, factor in factors.items():
        out[name] = (out[name] * factor).astype(out[name].dtype)
    return out
```

```python
import concourse.bass as bass
from concourse import mybir
from contextlib import ExitStack

F32 = mybir.dt.float32
F32R = mybir.dt.float32r
BF16 = mybir.dt.bfloat16
I32 = mybir.dt.int32
U32 = mybir.dt.uint32
ALU = mybir.AluOpType
ACT = mybir.ActivationFunctionType
AX = mybir.AxisListType

P = 128
B, T, D = 4, 512, 256
NT, DC = T // P, D // P
H, HD = 8, 128
S, XH, XE = 1024, 16, 16
SC = S // P
HG, NG = 4, 4
W = P // HG
E, F, K = 64, 128, 8
GR = 8
EPS = 1e-5
SELF_SCALE = float(HD) ** -0.5
CROSS_SCALE = float(XE) ** -0.5
ROUTED = 2.5
NEG = -1e30
REGION = B * T + P
TILES = B * T * K // P + E
P_AT = [P * i * (i + 1) // 2 for i in range(NT)]
PT_AT = [0, 512, 896, 1152]
TRI = P * NT * (NT + 1) // 2
BANK = 512
NORMS = 5
BLOCKS = 4
RING = 8
SLOTS = 4
LOADED = 8
FIELDS = 4
ROWS_IN = E * REGION + P
ROWS_OUT = TILES * P
FFN_LOADS = 5
CROSS_LOADS = 8 + 2 * DC + 3 * HG
FIRST_MAX_UNIT = 4
PARTS = TILES // (4 * B * 4)
PK = -(-K // PARTS)
HALF = K // 2
N_CONST = 8


class Signal:

    def __init__(self, sem, per_batch, step=1):
        self.sem, self.per_batch, self.step = sem, per_batch, step

    def value(self, b, k):
        return b * (self.per_batch * self.step) + k * self.step


def build(nc, a, out):
    ctx = ExitStack()
    with ctx:
        def sb(name, shape, dt=F32):
            return ctx.enter_context(nc.sbuf_tensor(name, shape, dt))

        def sem(name):
            return ctx.enter_context(nc.semaphore(name))

        def signal(name, per_batch, step=1):
            return Signal(sem(name), per_batch, step)

        X = sb("residual", [P, B * NT, D])
        attn_space = sb("attn_space", [P, H * T + DC * H * HD + H * D])
        wide = attn_space[:, 0:H * T]
        wq = attn_space[:, H * T:H * T + DC * H * HD].rearrange("p (c n) -> p c n", c=DC)
        wkv = sb("self_wkv", [P, DC, 2 * HD])
        wo = attn_space[:, H * T + DC * H * HD:].rearrange("p (h d) -> p h d", h=H)
        bq = sb("self_bq", [P, H])
        bkv = sb("self_bkv", [P, 2])
        peT = sb("position_t", [P, T])
        ident = sb("identity", [P, P])
        ident16 = sb("identity16", [P, P], BF16)
        causal16 = sb("causal16", [P, P], BF16)
        stats = sb("ln_stats", [P, SC, 6])
        mv = sb("ln_mean_var", [P, SC, 2])
        vep = sb("ln_var_eps", [P, SC])
        rstd = sb("ln_rstd", [P, SC])
        mhalf = sb("minus_half", [P, SC])
        scratch = sb("scratch", [P, 1])
        pool_scratch = sb("pool_scratch", [P, 1])
        carry = sb("pool_carry", [P, 2 * NT])
        pool_scratch2 = sb("pool_scratch2", [P, 1])
        C = sb("context", [P, SC, D])
        c_stats = sb("context_stats", [P, SC, 6])
        c_mv = sb("context_mean_var", [P, SC, 2])
        c_vep = sb("context_var_eps", [P, SC])
        c_rstd = sb("context_rstd", [P, SC])
        xwv = sb("cross_wv", [P, DC, D])
        xwo = sb("cross_wo", [P, DC, D])
        wq_g = sb("cross_wq_group", [P, DC, NG, P])
        wk_g = sb("cross_wk_group", [P, DC, NG, P])
        bq_g = sb("cross_bq_group", [P, NG])
        bk_g = sb("cross_bk_group", [P, NG])
        ones4 = sb("ones4", [HG, NG])
        norm_w = sb("norm_w", [P, DC])
        norm_b = sb("norm_b", [P, DC])
        norm1_w = sb("norm1_w", [P, DC])
        norm1_b = sb("norm1_b", [P, DC])
        bv_row = sb("cross_bv_row", [P, D])
        bo_row = sb("cross_bo_row", [P, D])
        VX = sb("cross_v", [P, SC, XH, XE + 1])
        k_hi = sb("k_hi", [P, S], F32R)
        k_lo = sb("k_lo", [P, S], F32R)
        q_hi = sb("q_hi", [P, T], F32R)
        q_lo = sb("q_lo", [P, T], F32R)
        m_hi = sb("max_hi", [P, T], F32R)
        m_lo = sb("max_lo", [P, T], F32R)
        KS = [sb(f"k_stack{i}", [P, HG, S], F32R) for i in range(2)]
        QS = [sb(f"q_stack{i}", [P, HG, T], F32R) for i in range(2)]
        MP = sb("max_halves", [P, 2, NT, HG])
        MX = sb("max_columns", [P, NT, HG, W])
        PX = [sb(f"cross_probs{i}", [P, 2, T]) for i in range(2)]
        q_whole = sb("q_whole", [P, T])
        QR = [sb(f"q_rows{i}", [P, XE, W]) for i in range(2)]
        OR = sb("out_rows", [P, XE, W])
        RG = sb("cross_row_inv", [P, XE])
        xn = sb("normed", [P, NT, D])
        xnT = sb("normed_t", [P, DC, T])
        QT = [sb(f"q_t{i}", [P, T]) for i in range(2)]
        KT = sb("k_t", [P, T])
        V = sb("v", [P, NT, HD])
        PR = [sb(f"probs{i}", [P, TRI]) for i in range(2)]
        PT = sb("probs_t", [P, TRI])
        OT = wide.rearrange("p (h t) -> p h t", h=H)
        CT = wide[:, 0:DC * S].rearrange("p (c s) -> p c s", c=DC)
        O = wide[:, DC * S:DC * S + NT * D].rearrange("p (i d) -> p i d", i=NT)
        mx = sb("row_max", [P, NT])
        nb = sb("exp_bias", [P, NT])
        rsum = sb("row_sum", [P, NT])
        rinv = sb("row_inv", [P, NT])

        wr = sb("router_w", [P, DC, E])
        br_row = sb("router_b_row", [P, E])
        ws_gu = sb("shared_gate_up", [P, DC, 2 * F])
        ws_d = sb("shared_down", [P, D])
        before16 = sb("before16", [P, P], BF16)
        ones16 = sb("ones16", [P, P], BF16)
        lower8 = sb("lower8", [P, GR, GR])
        region_i = PT[:, 0:E].bitcast(I32)
        region1 = sb("region1", [P, E])
        tile_i = sb("tile_i", [P, 2], I32)
        tile_no = sb("tile_no", [P, 2])
        xr = PX[0][:].rearrange("p a t -> p (a t)").rearrange("p (i d) -> p i d", d=D)
        def in_probs(which, n, inner):
            return PR[which][:, n * NT * E:(n + 1) * NT * E].rearrange(inner, i=NT, g=GR)

        SCR = in_probs(0, 0, "p (i g e) -> p i (g e)")
        SWB = in_probs(0, 1, "p (i g e) -> p i (g e)")
        SRT = in_probs(0, 2, "p (i g e) -> p i g e")
        CMP = in_probs(0, 3, "p (i g e) -> p i g e")
        CMQ = in_probs(0, 4, "p (i g e) -> p i g e")
        SEL = in_probs(1, 0, "p (i g e) -> p i (g e)")
        GS = sb("group_scores", [P, NT, GR])
        TOP = sb("top_scores", [P, NT, K])
        SEL16 = sb("selected16", [P, NT, E], BF16)
        WSUM = sb("weight_sum", [P, NT])
        CNT = sb("expert_counts", [P, E])
        def beside(col, n):
            return PR[1][:, NT * E + col:NT * E + col + n]

        BASE = beside(7 * E, E)
        V8 = sb("slots_sorted", [P, NT, K])
        IDXB = sb("batch_slots", [P, NT, K], U32)
        SLOT1 = sb("token_slots_1", [P, B * NT, PARTS * PK])
        IDX = sb("token_results", [P, B * NT, PARTS * PK], U32)
        WTS = sb("token_weights", [P, B * NT, K])
        ZERO = beside(8 * E, D)
        MOVE = beside(8 * E + D, PK * E).rearrange("p (j e) -> p j e", e=E)
        TF = beside(2 * E, E)
        TI = beside(3 * E, E).bitcast(I32)
        CUM = beside(4 * E, E)
        NEED = beside(5 * E, E).bitcast(I32)
        DD = BASE
        COUNT_I = beside(6 * E, E).bitcast(I32)
        IND = beside(0, 2 * E).rearrange("p (h e) -> p h e", h=2)
        TE = sb("tile_expert", [P, 2])
        TX = sb("tile_excess", [P, 2])
        TBF = sb("tile_fields_f", [P, 2, FIELDS])
        TB = sb("tile_fields", [P, 2, FIELDS], I32)
        TROW = PT[0:1, 0:2 * P * FIELDS].bitcast(I32)
        w_ring = attn_space[:, 0:RING * 3 * D].rearrange("p (s n) -> p s n", s=RING)
        SG = [attn_space[:, 6656 + i * F:6656 + (i + 1) * F] for i in range(2)]
        HH = [attn_space[:, 6912 + i * F:6912 + (i + 1) * F] for i in range(2)]
        HT = [attn_space[:, 7168 + i * P:7168 + (i + 1) * P] for i in range(2)]
        XS = [C[:, i, :] for i in range(LOADED)]
        XT = [PX[1][:].rearrange("p a t -> p (a t)")[:, i * D:(i + 1) * D] for i in range(SLOTS)]
        OS = [QR[i // 2][:].rearrange("p m w -> p (m w)")[:, (i % 2) * D:(i % 2 + 1) * D] for i in range(SLOTS)]
        OS2 = [QR[i][:].rearrange("p m w -> p (m w)").rearrange("p (i d) -> p i d", d=D) for i in range(2)]
        G = [C[:, j, :] for j in range(K)]
        EQ = QR[0][:].rearrange("p m w -> p (m w)").rearrange("p (j e) -> p j e", e=E)
        s_gate = q_whole[:]
        s_hid = OR[:].rearrange("p m w -> p (m w)")

        rows_in = nc.dram_tensor("rows_in", (ROWS_IN, D), F32, kind="Internal").ap()
        rows_out = nc.dram_tensor("rows_out", (ROWS_OUT, D), F32, kind="Internal").ap()
        table = nc.dram_tensor("tile_rows", (2 * P, FIELDS), I32, kind="Internal").ap()

        PS = ctx.enter_context(nc.psum_tensor("psum", [P, 8 * BANK], F32))

        def bank(n, lo=0, hi=BANK):
            return PS[:, n * BANK + lo:n * BANK + hi]

        S_PS = [bank(3, 384, 512), bank(4, 0, 256), bank(3, 0, 384), bank(2)]
        T_PS = [bank(5), bank(6, 0, 384), bank(1, 0, 256), bank(6, 384, 512)]

        ld_x = [sem(f"x_loaded{i}") for i in range(B)]
        ld_small = sem("small_loaded")
        ld_wqkv = sem("wqkv_loaded")
        ld_wo = sem("wo_loaded")
        s_const = sem("constants_made")
        s_const0 = sem("constants_cleared")
        s_batch = sem("batch_done")
        ld_ctx = signal("context_loaded", 1, 16)
        ld_cross = sem("cross_loaded")
        s_pad = sem("padded_cleared")
        s_vones = sem("ones_columns_set")
        s_cvar = signal("context_variance", 1)
        s_crstd = signal("context_rstd_ready", 1)
        s_cn = signal("context_normed", 1)
        s_cT = signal("context_transposed", 1)
        s_cTe = signal("context_t_ready", 1)
        s_vx = signal("cross_v_projected", 1)
        s_vxe = signal("cross_v_ready", 1)
        s_qw = signal("q_whole_ready", NG)
        s_qr = signal("q_rows_ready", NG)
        s_pk = [signal(f"group_k{i}_projected", NG) for i in range(2)]
        s_pq = signal("group_q_projected", NG)
        s_hi = signal("high_parts_ready", 3 * NG)
        s_lo = signal("low_parts_ready", 3 * NG)
        s_stack = [[signal(f"stack{i}_head{j}", NG // 2, 8 * 16) for j in range(HG)] for i in range(2)]
        s_p1 = signal("max_scores_ready", NG * NT * HG * 2)
        s_p1d = signal("max_scores_taken", NG * NT * HG * 2)
        s_mx = signal("max_ready", NG)
        s_mT = signal("max_transposed", NG)
        s_mh = signal("max_high_ready", NG)
        s_ml = signal("max_low_ready", NG)
        s_aug = signal("max_rows_stacked", NG, 8 * 16)
        s_st = signal("cross_scores_ready", NG * SC * 2)
        s_ex = signal("cross_exp_done", NG * SC * 2)
        s_pvx = signal("cross_pv_done", NG * SC * 2)
        s_or = signal("out_rows_taken", NG)
        s_o = signal("cross_out_ready", NG)
        s_xo = signal("cross_wo_projected", 1)
        s_out = sem("stored")
        s_dve = signal("dve_step", 1000)
        s_var = signal("variance_ready", NORMS)
        s_rstd = signal("rstd_ready", NORMS)
        s_xn = signal("normed_ready", BLOCKS)
        s_xnT = signal("normed_transposed", BLOCKS)
        s_xnTe = signal("normed_t_ready", BLOCKS)
        s_kv = signal("kv_projected", 1)
        s_kvd = signal("k_t_ready", 1)
        s_kva = signal("v_ready", 1)
        s_q = signal("q_projected", H)
        s_qe = signal("q_t_ready", H)
        s_s = signal("scores_ready", H)
        s_nb = signal("exp_bias_ready", H)
        s_exp = signal("exp_done", H)
        s_norm = signal("probs_ready", H)
        s_t = signal("probs_transposed", H)
        s_ptd = signal("probs_t_dve", H)
        s_pta = signal("probs_t_act", H)
        s_pv = signal("attn_ready", H)
        s_oe = signal("attn_t_ready", H)
        s_wo = signal("wo_projected", 1)

        ld_ffn = sem("ffn_loaded")
        s_zero = sem("zero_rows_ready")
        s_lg = signal("logits_ready", 1)
        s_gu = signal("shared_gate_up_ready", 1)
        s_ez = signal("logits_exp_ready", 1)
        s_sg = signal("shared_silu_ready", 1)
        s_sh = signal("shared_hidden_ready", 1)
        s_sd = signal("shared_out_ready", 1)
        s_sel = signal("experts_selected", 1)
        s_rk = signal("ranks_ready", 1)
        s_ix = signal("slots_ready", 1)
        s_scat = signal("rows_scattered", NT * K, 16)
        e_ld = [sem(f"tile_loaded{i}") for i in range(LOADED)]
        e_st = [sem(f"tiles_stored{i}") for i in range(2)]
        e_T = sem("tile_transposed")
        e_XT = sem("tile_t_ready")
        e_GU = sem("gate_up_ready")
        e_SG = sem("silu_ready")
        e_H = sem("hidden_ready")
        e_HP = sem("hidden_transposed")
        e_HT = sem("hidden_t_ready")
        e_D = sem("down_ready")
        e_O = sem("tile_out_ready")
        w_dma = [sem(f"weights_landing{i}") for i in range(2)]
        w_ready = sem("weights_ready")
        s_tab = sem("table_made")
        s_tabc = sem("table_step")
        s_idx = sem("result_row_step")
        s_tabd = sem("table_stored")
        s_tabl = sem("table_loaded")
        s_tabn = sem("table_zero_tile")
        g_ld = [sem(f"result_gathered{j}") for j in range(K)]
        g_use = sem("results_added")
        s_fin = sem("rows_finished")

        block = ctx.enter_context(nc.Block())

        @block.sync
        def _(sp):
            xv = a["x"].rearrange("b (i p) d -> b p i d", p=P)
            sp.dma_start(X[:, 0:NT, :], xv[0]).then_inc(ld_x[0], 16)
            sp.dma_start(wkv[:], a["L0_attn_Wkv"].rearrange("(c p) n -> p c n", p=P)).then_inc(ld_wqkv, 16)
            sp.dma_start(wq, a["L0_attn_Wq"].rearrange("(c p) n -> p c n", p=P)).then_inc(ld_wqkv, 16)
            sp.dma_start(peT[:], a["position_t"]).then_inc(ld_small, 16)
            sp.dma_start(bq[:], a["L0_attn_bq"].rearrange("(h p) -> p h", p=P), allow_slow_non_contiguous=True).then_inc(ld_small, 16)
            sp.dma_start(bkv[:], a["L0_attn_bkv"].rearrange("(h p) -> p h", p=P), allow_slow_non_contiguous=True).then_inc(ld_small, 16)
            sp.dma_start(wo, a["L0_attn_Wo"].rearrange("(h p) n -> p h n", p=P)).then_inc(ld_wo, 16)
            for i in range(1, B):
                sp.dma_start(X[:, i * NT:(i + 1) * NT, :], xv[i]).then_inc(ld_x[i], 16)

            def stack(b, g):
                sp.wait_ge(s_lo.sem, s_lo.value(b, 3 * g + 3))
                for j in range(HG):
                    done = s_stack[g % 2][j].sem
                    for t, (kp, qp) in enumerate(((k_hi, q_hi), (k_lo, q_hi), (k_hi, q_lo), (k_lo, q_lo))):
                        rows, head = slice(W * t, W * t + W), slice(W * j, W * j + W)
                        sp.dma_start(KS[g % 2][rows, j, :].bitcast(F32), kp[head, :].bitcast(F32)).then_inc(done, 16)
                        sp.dma_start(QS[g % 2][rows, j, :].bitcast(F32), qp[head, :].bitcast(F32)).then_inc(done, 16)

            def stack_max(b, g):
                sp.wait_ge(s_mh.sem, s_mh.value(b, g + 1))
                for j in range(HG):
                    sp.dma_start(QS[g % 2][XE:XE + 1, j, :].bitcast(F32),
                                 m_hi[W * j + XE:W * j + XE + 1, :].bitcast(F32)).then_inc(s_aug.sem, 16)
                sp.wait_ge(s_ml.sem, s_ml.value(b, g + 1))
                for j in range(HG):
                    sp.dma_start(QS[g % 2][2 * W + XE:2 * W + XE + 1, j, :].bitcast(F32),
                                 m_lo[W * j + XE:W * j + XE + 1, :].bitcast(F32)).then_inc(s_aug.sem, 16)

            sp.dma_start(norm_w[:], a["L0_xattn_norm_w"].rearrange("(c p) -> p c", p=P), allow_slow_non_contiguous=True).then_inc(ld_cross, 16)
            sp.dma_start(norm_b[:], a["L0_xattn_norm_b"].rearrange("(c p) -> p c", p=P), allow_slow_non_contiguous=True).then_inc(ld_cross, 16)
            sp.dma_start(norm1_w[:], a["L0_xattn_norm1_w"].rearrange("(c p) -> p c", p=P), allow_slow_non_contiguous=True).then_inc(ld_cross, 16)
            sp.dma_start(norm1_b[:], a["L0_xattn_norm1_b"].rearrange("(c p) -> p c", p=P), allow_slow_non_contiguous=True).then_inc(ld_cross, 16)
            sp.dma_start(bv_row[:], a["L0_xattn_bv"].partition_broadcast(P)).then_inc(ld_cross, 16)
            sp.dma_start(bo_row[:], a["L0_xattn_bo"].partition_broadcast(P)).then_inc(ld_cross, 16)
            sp.dma_start(xwv[:], a["L0_xattn_Wv"].rearrange("(c p) n -> p c n", p=P)).then_inc(ld_cross, 16)
            sp.dma_start(xwo[:], a["L0_xattn_Wo"].rearrange("(c p) n -> p c n", p=P)).then_inc(ld_cross, 16)
            sp.wait_ge(s_pad, 5)
            for c in range(DC):
                for w_g, w in ((wq_g, a["L0_xattn_Wq"]), (wk_g, a["L0_xattn_Wk"])):
                    sp.dma_start(w_g[:, c, :, :].rearrange("p g (j w) -> p (g j) w", j=HG)[:, :, 0:XE],
                                 w[c * P:(c + 1) * P, :].rearrange("p (h e) -> p h e", e=XE)).then_inc(ld_cross, 16)
            for j in range(HG):
                for b_g, v in ((bq_g, a["L0_xattn_bq"]), (bk_g, a["L0_xattn_bk"])):
                    sp.dma_start(b_g[W * j:W * j + XE, :], v.rearrange("(g j e) -> j e g", j=HG, e=XE)[j],
                                 allow_slow_non_contiguous=True).then_inc(ld_cross, 16)
                sp.dma_start(bk_g[W * j + XE:W * j + XE + 1, :], ones4[j:j + 1, :]).then_inc(ld_cross, 16)

            sp.dma_start(wr[:], a["L0_ffn_w_router"].rearrange("(c p) n -> p c n", p=P)).then_inc(ld_ffn, 16)
            sp.dma_start(br_row[:], a["L0_ffn_b_router"].partition_broadcast(P)).then_inc(ld_ffn, 16)
            sp.dma_start(ws_gu[:, :, 0:F], a["L0_ffn_ws_gate"].rearrange("(c p) n -> p c n", p=P)).then_inc(ld_ffn, 16)
            sp.dma_start(ws_gu[:, :, F:2 * F], a["L0_ffn_ws_up"].rearrange("(c p) n -> p c n", p=P)).then_inc(ld_ffn, 16)
            sp.dma_start(ws_d[:], a["L0_ffn_ws_down"]).then_inc(ld_ffn, 16)

            with sp.Fori(0, B) as b:
                stack(b, 0)
                for g in range(NG):
                    stack_max(b, g)
                    if g + 1 < NG:
                        stack(b, g + 1)

            sp.wait_ge(s_tab, 1)
            sp.dma_start(table.rearrange("(h p) f -> p h f", h=2), TB[:]).then_inc(s_tabd, 16)
            sp.wait_ge(s_tabd, 16)
            sp.dma_start(TROW, table.rearrange("(o t) f -> o (t f)", o=1)).then_inc(s_tabl, 16)
            sp.wait_ge(s_tabl, 16)
            sp.dma_start(rows_in[E * REGION:ROWS_IN, :], ZERO).then_inc(s_zero, 16)
            sp.wait_ge(s_scat.sem, s_scat.value(B, 1))

            gate, up, down = a["L0_ffn_we_gate"], a["L0_ffn_we_up"], a["L0_ffn_we_down"]

            def load_expert(e, slot, parity):
                w = w_ring[:, slot, 0:4 * F].rearrange("p (c n) -> p c n", c=DC)
                last_row = sp.value_load(COUNT_I[0:1, bass.ds(e, 1)], min_val=0, max_val=B * T)
                sp.dma_start(w[:, :, 0:F], gate[e].rearrange("(c p) n -> p c n", p=P)).then_inc(w_dma[parity], 16)
                sp.dma_start(w[:, :, F:2 * F], up[e].rearrange("(c p) n -> p c n", p=P)).then_inc(w_dma[parity], 16)
                sp.dma_start(w_ring[:, slot, 4 * F:4 * F + D], down[e]).then_inc(w_dma[parity], 16)
                sp.dma_start(rows_in[bass.ds(e * REGION + last_row, P), :], ZERO).then_inc(w_dma[parity], 16)

            def landed(parity, value):
                sp.wait_ge(w_dma[parity], value)
                nc.sync.sem_inc(w_ready, 1)

            for e in range(RING):
                if e:
                    landed((e - 1) % 2, 64 * ((e - 1) // 2 + 1))
                load_expert(e, e, e % 2)
            with sp.Fori(1, E // RING) as n:
                for u in range(RING):
                    need = sp.value_load(NEED[0:1, bass.ds(n * RING + u - RING, 1)], min_val=1, max_val=TILES + 1)
                    landed((u + 1) % 2, n * (64 * RING // 2) + 64 * ((u + 1) // 2))
                    sp.wait_ge(e_D, need)
                    load_expert(n * RING + u, u, u % 2)
            landed((E - 1) % 2, 64 * E // 2)

            ov = out.rearrange("b (i p) d -> (b i) p d", p=P)
            with sp.Fori(0, B * NT) as t:
                sp.wait_ge(s_fin, t + 1)
                sp.dma_start(ov[t], X[:, t, :]).then_inc(s_out, 16)
            sp.wait_ge(s_out, B * NT * 16)

        @block.gpsimd
        def _(pool):
            nc.gpsimd.memset(ident[:], 0.0).then_inc(s_const0, 1)
            nc.gpsimd.memset(causal16[:], 0.0).then_inc(s_const0, 1)
            nc.gpsimd.memset(mhalf[:], -0.5).then_inc(s_const, 1)
            nc.gpsimd.memset(wq_g[:], 0.0).then_inc(s_pad, 1)
            nc.gpsimd.memset(wk_g[:], 0.0).then_inc(s_pad, 1)
            nc.gpsimd.memset(bq_g[:], 0.0).then_inc(s_pad, 1)
            nc.gpsimd.memset(bk_g[:], 0.0).then_inc(s_pad, 1)
            nc.gpsimd.memset(ones4[:], 1.0).then_inc(s_pad, 1)
            nc.gpsimd.memset(VX[:, :, :, XE:XE + 1], 1.0).then_inc(s_vones, 1)
            nc.gpsimd.memset(MX[:], 0.0).then_inc(s_vones, 1)
            pool.wait_ge(s_const0, 2)
            nc.gpsimd.affine_select(out=ident[:], in_=ident[:], compare_op=ALU.not_equal, fill=1.0,
                                    base=0, pattern=[[-1, P]], channel_multiplier=1).then_inc(s_const, 1)
            nc.gpsimd.affine_select(out=causal16[:], in_=causal16[:], compare_op=ALU.is_ge, fill=NEG,
                                    base=0, pattern=[[-1, P]], channel_multiplier=1).then_inc(s_const, 1)
            nc.gpsimd.memset(ones16[:], 1.0).then_inc(s_const, 1)
            nc.gpsimd.memset(lower8[:], 1.0).then_inc(s_const0, 1)
            nc.gpsimd.memset(before16[:], 1.0).then_inc(s_const0, 1)
            nc.gpsimd.iota(region_i, pattern=[[REGION, E]], base=1, channel_multiplier=0).then_inc(s_const0, 1)
            nc.gpsimd.iota(tile_i[:], pattern=[[P, 2]], base=0, channel_multiplier=1).then_inc(s_const0, 1)
            pool.wait_ge(s_const, 3)
            nc.gpsimd.tensor_copy(ident16[:], ident[:]).then_inc(s_const, 1)
            pool.wait_ge(s_const0, 6)
            nc.gpsimd.affine_select(out=lower8[:], in_=lower8[:], compare_op=ALU.is_gt, fill=0.0,
                                    base=0, pattern=[[1, GR], [-1, GR]], channel_multiplier=0).then_inc(s_const, 1)
            nc.gpsimd.affine_select(out=before16[:], in_=before16[:], compare_op=ALU.is_gt, fill=0.0,
                                    base=0, pattern=[[1, P]], channel_multiplier=-1).then_inc(s_const, 1)
            nc.gpsimd.tensor_copy(region1[:], region_i).then_inc(s_const, 1)
            nc.gpsimd.tensor_copy(tile_no[:], tile_i[:]).then_inc(s_const0, 1)
            nc.gpsimd.memset(CNT[:], 0.0).then_inc(s_const0, 1)
            pool.dma_start(table[0:P, 0:2], tile_i[:]).then_inc(s_scat.sem, 16)
            with pool.Fori(0, B) as b:
                pool.wait_ge(s_var.sem, s_var.value(b, 1))
                nc.gpsimd.tensor_tensor(rstd[:, 0:NT], vep[:, 0:NT], mhalf[:, 0:NT], ALU.pow).then_inc(s_rstd.sem, 1)
                pool.wait_ge(s_cvar.sem, s_cvar.value(b, 1))
                nc.gpsimd.tensor_tensor(c_rstd[:], c_vep[:], mhalf[:], ALU.pow).then_inc(s_crstd.sem, 1)
                pool.wait_ge(s_crstd.sem, s_crstd.value(b, 1))
                nc.gpsimd.tensor_tensor(pool_scratch[:], mhalf[:, 0:1], mhalf[:, 0:1], ALU.mult)
                for i in range(SC):
                    last = nc.gpsimd.tensor_scalar(C[:, i, :], C[:, i, :], c_mv[:, i, 0:1], c_rstd[:, i:i + 1],
                                                   ALU.subtract, ALU.mult)
                last.then_inc(s_cn.sem, 1)
                for n in range(1, NORMS):
                    pool.wait_ge(s_var.sem, s_var.value(b, n + 1))
                    nc.gpsimd.tensor_tensor(rstd[:, 0:NT], vep[:, 0:NT], mhalf[:, 0:NT], ALU.pow).then_inc(s_rstd.sem, 1)
                pool.wait_ge(s_ix.sem, s_ix.value(b, 1))
                nc.gpsimd.tensor_tensor(pool_scratch2[:], mhalf[:, 0:1], mhalf[:, 0:1], ALU.mult)
                for i in range(NT):
                    for j in range(K):
                        nc.gpsimd.indirect_dma_start(
                            out=rows_in, out_offset=bass.IndirectOffsetOnAxis(ap=IDXB[:, i, j:j + 1], axis=0),
                            in_=xr[:, i, :], in_offset=None).then_inc(s_scat.sem, 16)

            with pool.Fori(0, TILES // SLOTS) as n:
                for u in range(0, SLOTS, 2):
                    t = n * SLOTS + u
                    pool.wait_ge(e_O, t + 2 + 2)
                    pool.dma_start(rows_out[bass.ds(t * P, 2 * P), :].rearrange("(i p) d -> p i d", p=P),
                                   OS2[u // 2]).then_inc(e_st[u // 2], 16)

            for i in range(2):
                pool.wait_ge(e_st[i], 16 * (TILES // SLOTS))
            pool.wait_ge(e_T, TILES + 4)
            nc.gpsimd.sem_inc(g_use, K)
            pool.wait_ge(s_idx, 4 * B * NT * PARTS)
            with pool.Fori(0, B) as n:
                pool.wait_ge(g_use, n * (NT * K) + K)
                nc.gpsimd.tensor_copy(IDXB[:], IDX[:, bass.ds(n * NT, NT), 0:K]).then_inc(s_tabn, 1)
                pool.wait_ge(s_tabn, n + 1)
                for i in range(NT):
                    for j in range(K):
                        if j % HALF == 0:
                            at = 2 * i + j // HALF
                            pool.wait_ge(g_use, n * (NT * K) + i * K + j + HALF)
                            nc.gpsimd.tensor_tensor(carry[:, at:at + 1], mhalf[:, 0:1], mhalf[:, 0:1], ALU.mult)
                        nc.gpsimd.indirect_dma_start(
                            out=G[j], out_offset=None, in_=rows_out,
                            in_offset=bass.IndirectOffsetOnAxis(ap=IDXB[:, i, j:j + 1], axis=0)).then_inc(g_ld[j], 16)

        @block.scalar
        def _(act):
            act.wait_ge(ld_small, 48)
            act.wait_ge(ld_cross, CROSS_LOADS * 16)
            context = a["ctx_1024"].rearrange("b (i p) d -> b p i d", p=P)
            with act.Fori(0, B) as b:
                act.wait_ge(s_batch, b + 1)
                act.dma_start(C[:], context[b]).then_inc(ld_ctx.sem, 16)
                act.wait_ge(s_kv.sem, s_kv.value(b, 1))
                nc.scalar.copy(V[:].rearrange("p i d -> p (i d)"), bank(1)).then_inc(s_kva.sem, 1)

                def probs_t(h):
                    act.wait_ge(s_t.sem, s_t.value(b, h + 1))
                    if h:
                        act.wait_ge(s_pv.sem, s_pv.value(b, h))
                    for j in (1, 2, 3):
                        n = T - P * j
                        last = nc.scalar.copy(PT[:, PT_AT[j]:PT_AT[j] + n], T_PS[j])
                    last.then_inc(s_pta.sem, 1)

                def attn_t(h):
                    act.wait_ge(s_pv.sem, s_pv.value(b, h + 1))
                    nc.scalar.activation(OT[:, h, :], bank(7), ACT.Identity, bias=bkv[:, 1:2]).then_inc(s_oe.sem, 1)

                for h in range(H):
                    if h:
                        probs_t(h - 1)
                    act.wait_ge(s_nb.sem, s_nb.value(b, h + 1))
                    if h >= 2:
                        act.wait_ge(s_t.sem, s_t.value(b, h - 1))
                    for i in range(NT):
                        n = P * (i + 1)
                        last = nc.scalar.activation(PR[h % 2][:, P_AT[i]:P_AT[i] + n], S_PS[i], ACT.Exp,
                                                    bias=nb[:, i:i + 1], scale=SELF_SCALE,
                                                    accum_out=rsum[:, i:i + 1])
                    last.then_inc(s_exp.sem, 1)
                    if h:
                        attn_t(h - 1)
                probs_t(H - 1)
                attn_t(H - 1)

                act.wait_ge(s_cT.sem, s_cT.value(b, 1))
                for c in range(DC):
                    last = nc.scalar.activation(CT[:, c, :], PS[:, 2 * c * BANK:2 * (c + 1) * BANK], ACT.Identity,
                                                bias=norm_b[:, c:c + 1], scale=norm_w[:, c:c + 1])
                last.then_inc(s_cTe.sem, 1)

                def high_parts(g):
                    if g:
                        for j in range(HG):
                            st = s_stack[(g - 1) % 2][j]
                            act.wait_ge(st.sem, st.value(b, (g - 1) // 2 + 1))
                    for half in range(2):
                        act.wait_ge(s_pk[half].sem, s_pk[half].value(b, g + 1))
                        nc.scalar.activation(k_hi[:, half * T:(half + 1) * T], bank(half), ACT.Identity,
                                             bias=bk_g[:, g:g + 1]).then_inc(s_hi.sem, 1)
                    act.wait_ge(s_pq.sem, s_pq.value(b, g + 1))
                    nc.scalar.activation(q_hi[:], bank(7), ACT.Identity, bias=bq_g[:, g:g + 1]).then_inc(s_hi.sem, 1)
                    if g:
                        act.wait_ge(s_qr.sem, s_qr.value(b, g))
                    nc.scalar.activation(q_whole[:], bank(7), ACT.Identity, bias=bq_g[:, g:g + 1]).then_inc(s_qw.sem, 1)

                def max_high(g):
                    act.wait_ge(s_mT.sem, s_mT.value(b, g + 1))
                    if g:
                        act.wait_ge(s_aug.sem, s_aug.value(b, g))
                    nc.scalar.mul(m_hi[:], bank(2), -1.0).then_inc(s_mh.sem, 1)

                act.wait_ge(s_scat.sem, s_scat.value(b, 1))
                high_parts(0)
                for g in range(NG):
                    max_high(g)
                    if g + 1 < NG:
                        high_parts(g + 1)
                    for u in range(SC * 2):
                        n = g * SC * 2 + u
                        act.wait_ge(s_st.sem, s_st.value(b, n + 1))
                        if n >= 2:
                            act.wait_ge(s_pvx.sem, s_pvx.value(b, n - 1))
                        pair = PS[:, (2 + 2 * (u % 2)) * BANK:(4 + 2 * (u % 2)) * BANK]
                        nc.scalar.activation(PX[u % 2][:].rearrange("p j l -> p (j l)"), pair, ACT.Exp,
                                             scale=CROSS_SCALE).then_inc(s_ex.sem, 1)

                act.wait_ge(s_lg.sem, s_lg.value(b, 1))
                nc.scalar.activation(SCR.rearrange("p i e -> p (i e)"), bank(0, 0, NT * E), ACT.Exp,
                                     scale=-1.0).then_inc(s_ez.sem, 1)
                act.wait_ge(s_gu.sem, s_gu.value(b, 1))
                nc.scalar.activation(s_gate, bank(2), ACT.Silu).then_inc(s_sg.sem, 1)

            act.wait_ge(s_tabl, 16)
            act.wait_ge(s_zero, 16)
            nc.scalar.sem_inc(e_O, 2)

            def load_tile(t, slot):
                row = act.value_load(TROW[0:1, bass.ds(t * FIELDS, 1)], min_val=0, max_val=E * REGION)
                expert = act.value_load(TROW[0:1, bass.ds(t * FIELDS + 3, 1)], min_val=0, max_val=E)
                act.wait_ge(w_ready, expert)
                act.dma_start(XS[slot], rows_in[bass.ds(row, P), :]).then_inc(e_ld[slot], 16)

            def silu(t, u):
                act.wait_ge(e_GU, t + 1)
                nc.scalar.activation(SG[u % 2], bank(2 + u % 2, 0, F), ACT.Silu).then_inc(e_SG, 1)

            def hidden_t(t, u):
                act.wait_ge(e_HP, t + 1)
                nc.scalar.copy(HT[u % 2], bank(4 + u % 2, 0, P)).then_inc(e_HT, 1)

            def act_tiles(n, first=False, last=False):
                for u in range(LOADED):
                    t = n * LOADED + u
                    silu(t + 2, u)
                    if not last or u < 4:
                        load_tile(t + LOADED, u)
                    hidden_t(t + 1, u + 1)
                    act.wait_ge(e_D, t + 2)
                    turn, v = n * (LOADED // SLOTS) + u // SLOTS, u % SLOTS
                    if v % 2 == 0 and not (first and u < SLOTS):
                        act.wait_ge(e_st[v // 2], turn * 16)
                    nc.scalar.copy(OS[v], bank(6 + u % 2, 0, D)).then_inc(e_O, 1)

            for t in range(LOADED):
                load_tile(t, t)
            silu(0, 0)
            silu(1, 1)
            hidden_t(0, 0)
            act_tiles(0, first=True)
            with act.Fori(1, TILES // LOADED - 1) as n:
                act_tiles(n)
            act_tiles(TILES // LOADED - 1, last=True)

        @block.vector
        def _(dve):
            dve.wait_ge(s_const, N_CONST)
            dve.wait_ge(ld_small, 48)
            dve.wait_ge(ld_cross, CROSS_LOADS * 16)
            dve.wait_ge(s_vones, 2)
            dve.wait_ge(s_const0, 8)
            dve.wait_ge(ld_ffn, FFN_LOADS * 16)
            nc.vector.sem_inc(s_batch, 1)
            for i in range(B):
                dve.wait_ge(ld_x[i], 16)
            with dve.Fori(0, B) as b:
                n_links = [0]

                def link(ins):
                    n_links[0] += 1
                    ins.then_inc(s_dve.sem, 1)

                def linked():
                    dve.wait_ge(s_dve.sem, s_dve.value(b, n_links[0]))

                def settle():
                    linked()
                    link(nc.vector.memset(scratch[:], 0.0))

                norms = [0]

                def row_norm(src, dst, tiles=NT):
                    norms[0] += 1
                    for i in range(tiles):
                        link(nc.vector.bn_stats(stats[:, i, :], src(i)))
                    settle()
                    for i in range(tiles):
                        link(nc.vector.bn_aggr(mv[:, i, :], stats[:, i, :]))
                    linked()
                    nc.vector.tensor_scalar(vep[:, 0:tiles], mv[:, 0:tiles, 1], EPS, None, ALU.add).then_inc(s_var.sem, 1)
                    dve.wait_ge(s_rstd.sem, s_rstd.value(b, norms[0]))
                    for i in range(tiles):
                        last = nc.vector.tensor_scalar(dst(i), src(i), mv[:, i, 0:1], rstd[:, i:i + 1],
                                                       ALU.subtract, ALU.mult)
                    return last

                def x_row(i):
                    return X[:, b * NT + i, :]

                def xn_row(i):
                    return xn[:, i, :]

                row_norm(x_row, xn_row).then_inc(s_xn.sem, 1)
                dve.wait_ge(ld_ctx.sem, ld_ctx.value(b, 1))
                for i in range(SC):
                    link(nc.vector.bn_stats(c_stats[:, i, :], C[:, i, :]))
                settle()
                for i in range(SC):
                    link(nc.vector.bn_aggr(c_mv[:, i, :], c_stats[:, i, :]))
                linked()
                nc.vector.tensor_scalar(c_vep[:], c_mv[:, :, 1], EPS, None, ALU.add).then_inc(s_cvar.sem, 1)
                dve.wait_ge(s_xnT.sem, s_xnT.value(b, 1))
                nc.vector.tensor_copy(xnT[:].rearrange("p c t -> p (c t)"), PS[:, 5 * BANK:7 * BANK]).then_inc(s_xnTe.sem, 1)
                dve.wait_ge(s_kv.sem, s_kv.value(b, 1))
                nc.vector.scalar_tensor_tensor(KT[:], bank(7), bkv[:, 0:1], peT[:], ALU.add, ALU.add).then_inc(s_kvd.sem, 1)

                def q_t(h):
                    dve.wait_ge(s_q.sem, s_q.value(b, h + 1))
                    if h >= 2:
                        dve.wait_ge(s_s.sem, s_s.value(b, h - 1))
                    nc.vector.scalar_tensor_tensor(QT[h % 2][:], bank(0), bq[:, h:h + 1], peT[:],
                                                   ALU.add, ALU.add).then_inc(s_qe.sem, 1)

                def probs_t(h):
                    dve.wait_ge(s_t.sem, s_t.value(b, h + 1))
                    if h:
                        dve.wait_ge(s_pv.sem, s_pv.value(b, h))
                    nc.vector.tensor_copy(PT[:, 0:T], T_PS[0]).then_inc(s_ptd.sem, 1)

                q_t(0)
                for h in range(H):
                    dve.wait_ge(s_s.sem, s_s.value(b, h + 1))
                    for i in range(NT):
                        link(nc.vector.tensor_reduce(mx[:, i:i + 1], S_PS[i], AX.X, ALU.max))
                    linked()
                    nc.vector.tensor_scalar(nb[:], mx[:], -SELF_SCALE, None, ALU.mult).then_inc(s_nb.sem, 1)
                    if h:
                        probs_t(h - 1)
                    if h + 1 < H:
                        q_t(h + 1)
                    dve.wait_ge(s_exp.sem, s_exp.value(b, h + 1))
                    link(nc.vector.reciprocal(rinv[:], rsum[:]))
                    linked()
                    for i in range(NT):
                        rows = PR[h % 2][:, P_AT[i]:P_AT[i] + P * (i + 1)]
                        last = nc.vector.tensor_scalar(rows, rows, rinv[:, i:i + 1], None, ALU.mult)
                    last.then_inc(s_norm.sem, 1)
                probs_t(H - 1)
                dve.wait_ge(s_wo.sem, s_wo.value(b, 1))
                for i in range(NT):
                    last = nc.vector.tensor_tensor(X[:, b * NT + i, :], X[:, b * NT + i, :],
                                                   bank(2 + i // 2, (i % 2) * D, (i % 2) * D + D), ALU.add)
                    link(last)
                settle()

                link(row_norm(x_row, xn_row))
                linked()
                row_norm(xn_row, xn_row).then_inc(s_xn.sem, 1)

                def affine(first, w, bias):
                    for c in range(DC):
                        last = nc.vector.tensor_scalar(xnT[:, c, :], bank(first + c), w[:, c:c + 1], bias[:, c:c + 1],
                                                       ALU.mult, ALU.add)
                    last.then_inc(s_xnTe.sem, 1)

                dve.wait_ge(s_xnT.sem, s_xnT.value(b, 2))
                affine(4, norm_w, norm_b)
                dve.wait_ge(s_vx.sem, s_vx.value(b, 1))
                for n in range(4):
                    for i in range(2):
                        last = nc.vector.tensor_tensor(VX[:, 2 * n + i, :, 0:XE],
                                                       bank(n, i * D, i * D + D).rearrange("p (h e) -> p h e", e=XE),
                                                       bv_row[:].rearrange("p (h e) -> p h e", e=XE), ALU.add)
                last.then_inc(s_vxe.sem, 1)
                def low_parts(g):
                    for half in range(2):
                        dve.wait_ge(s_hi.sem, s_hi.value(b, 3 * g + half + 1))
                        cols = slice(half * T, (half + 1) * T)
                        nc.vector.scalar_tensor_tensor(k_lo[:, cols], bank(half), bk_g[:, g:g + 1],
                                                       k_hi[:, cols].bitcast(F32), ALU.add, ALU.subtract).then_inc(s_lo.sem, 1)
                    dve.wait_ge(s_qw.sem, s_qw.value(b, g + 1))
                    nc.vector.tensor_tensor(q_lo[:], q_whole[:], q_hi[:].bitcast(F32), ALU.subtract).then_inc(s_lo.sem, 1)
                    if g >= 2:
                        dve.wait_ge(s_o.sem, s_o.value(b, g - 1))
                    nc.vector.transpose(QR[g % 2][:], q_whole[:].rearrange("p (q m) -> p m q", m=XE)).then_inc(s_qr.sem, 1)

                def maxima(g, n):
                    j, i, half = n // (2 * NT), n // 2 % NT, n % 2
                    k = g * 2 * NT * HG + n
                    dve.wait_ge(s_p1.sem, s_p1.value(b, k + 1))
                    nc.vector.tensor_reduce(MP[:, half, i, j:j + 1], bank(k % 2), AX.X, ALU.max).then_inc(s_p1d.sem, 1)

                def max_columns(g):
                    dve.wait_ge(s_p1d.sem, s_p1d.value(b, (g + 1) * 2 * NT * HG))
                    if g:
                        dve.wait_ge(s_mT.sem, s_mT.value(b, g))
                    nc.vector.tensor_tensor(MX[:, :, :, XE], MP[:, 0], MP[:, 1], ALU.max).then_inc(s_mx.sem, 1)

                def max_low(g):
                    dve.wait_ge(s_mh.sem, s_mh.value(b, g + 1))
                    nc.vector.scalar_tensor_tensor(m_lo[:], bank(2), -1.0, m_hi[:].bitcast(F32),
                                                   ALU.mult, ALU.subtract).then_inc(s_ml.sem, 1)

                def out_rows(g):
                    dve.wait_ge(s_pvx.sem, s_pvx.value(b, (g + 1) * SC * 2))
                    nc.vector.transpose(OR[:], bank(6).rearrange("p (q m) -> p m q", m=XE)).then_inc(s_or.sem, 1)
                    dve.wait_ge(s_or.sem, s_or.value(b, g + 1))
                    link(nc.vector.reciprocal(RG[:], OR[:, :, XE]))
                    linked()
                    mine = O[:, g, :].rearrange("p (m e) -> p m e", e=XE)
                    link(nc.vector.tensor_tensor(mine, OR[:, :, 0:XE],
                                                 RG[:].unsqueeze(2).to_broadcast([P, XE, XE]), ALU.mult))
                    linked()
                    nc.vector.tensor_tensor(mine, mine, QR[g % 2][:, :, 0:XE], ALU.add).then_inc(s_o.sem, 1)

                low_parts(0)
                for n in range(2 * NT * HG):
                    maxima(0, n)
                for g in range(NG):
                    max_columns(g)
                    max_low(g)
                    if g:
                        out_rows(g - 1)
                    if g + 1 < NG:
                        low_parts(g + 1)
                    if g + 1 < NG:
                        for n in range(2 * NT * HG):
                            maxima(g + 1, n)
                out_rows(NG - 1)
                dve.wait_ge(s_o.sem, s_o.value(b, NG))
                row_norm(lambda i: O[:, i, :], xn_row).then_inc(s_xn.sem, 1)
                for i in range(NT):
                    link(nc.vector.tensor_tensor(O[:, i, :], O[:, i, :], bo_row[:], ALU.add))
                dve.wait_ge(s_xnT.sem, s_xnT.value(b, 3))
                affine(4, norm1_w, norm1_b)
                linked()
                for i in range(NT):
                    link(nc.vector.tensor_tensor(x_row(i), x_row(i), O[:, i, :], ALU.add))
                linked()
                dve.wait_ge(s_xo.sem, s_xo.value(b, 1))
                for i in range(NT):
                    link(nc.vector.tensor_tensor(x_row(i), x_row(i),
                                                 bank(2 + i // 2, (i % 2) * D, (i % 2) * D + D), ALU.add))

                dve.wait_ge(s_scat.sem, s_scat.value(b, 1))
                settle()
                row_norm(x_row, lambda i: xr[:, i, :]).then_inc(s_xn.sem, 1)
                dve.wait_ge(s_xnT.sem, s_xnT.value(b, 4))
                nc.vector.tensor_copy(xnT[:].rearrange("p c t -> p (c t)"), PS[:, 4 * BANK:6 * BANK]).then_inc(s_xnTe.sem, 1)

                def each(ap):
                    return ap.rearrange("p i e -> p (i e)")

                def over_tiles(row):
                    return row.unsqueeze(1).to_broadcast([P, NT, E])

                dve.wait_ge(s_ez.sem, s_ez.value(b, 1))
                link(nc.vector.tensor_scalar(each(SWB), each(SCR), 1.0, None, ALU.add))
                linked()
                link(nc.vector.reciprocal(each(SCR), each(SWB)))
                linked()
                link(nc.vector.tensor_tensor(SWB, SCR, over_tiles(br_row[:]), ALU.add))
                settle()
                for i in range(NT):
                    for g in range(E // GR):
                        link(nc.vector.max(SRT[:, i, g, :], SWB[:, i, g * GR:(g + 1) * GR]))
                linked()
                link(nc.vector.tensor_tensor(GS[:], SRT[:, :, :, 0], SRT[:, :, :, 1], ALU.add))
                linked()
                other = GS[:].unsqueeze(2).to_broadcast([P, NT, GR, GR])
                own = GS[:].unsqueeze(3).to_broadcast([P, NT, GR, GR])
                link(nc.vector.tensor_tensor(CMP, other, own, ALU.is_gt))
                link(nc.vector.tensor_tensor(CMQ, other, own, ALU.is_equal))
                linked()
                link(nc.vector.tensor_tensor(CMQ, CMQ, lower8[:].unsqueeze(1).to_broadcast([P, NT, GR, GR]), ALU.mult))
                linked()
                link(nc.vector.tensor_tensor(CMP, CMP, CMQ, ALU.add))
                linked()
                link(nc.vector.tensor_reduce(GS[:], CMP, AX.X, ALU.add))
                linked()
                link(nc.vector.tensor_scalar(GS[:], GS[:], 3.5, None, ALU.is_lt))
                linked()
                grouped = SWB.rearrange("p i (g e) -> p i g e", e=GR)
                link(nc.vector.tensor_tensor(grouped, grouped, GS[:].unsqueeze(3).to_broadcast([P, NT, GR, GR]), ALU.mult))
                settle()
                for i in range(NT):
                    link(nc.vector.max(TOP[:, i, :], SWB[:, i, :]))
                settle()
                for i in range(NT):
                    link(nc.vector.match_replace(SEL[:, i, :], TOP[:, i, :], SWB[:, i, :], NEG))
                linked()
                link(nc.vector.tensor_scalar(each(SEL), each(SEL), NEG / 10, None, ALU.is_lt))
                linked()
                nc.vector.tensor_copy(each(SEL16[:]), each(SEL)).then_inc(s_sel.sem, 1)
                link(nc.vector.tensor_tensor(SCR, SCR, SEL, ALU.mult))
                linked()
                link(nc.vector.tensor_reduce(WSUM[:], SCR, AX.X, ALU.add))
                linked()
                link(nc.vector.tensor_scalar(WSUM[:], WSUM[:], 1e-20, None, ALU.add))
                linked()
                link(nc.vector.reciprocal(WSUM[:], WSUM[:]))
                linked()
                link(nc.vector.tensor_scalar(WSUM[:], WSUM[:], ROUTED, None, ALU.mult))
                linked()
                link(nc.vector.tensor_tensor(SCR, SCR, WSUM[:].unsqueeze(2).to_broadcast([P, NT, E]), ALU.mult))
                link(nc.vector.tensor_tensor(BASE, CNT[:], region1[:], ALU.add))
                linked()
                dve.wait_ge(s_rk.sem, s_rk.value(b, 1))
                link(nc.vector.tensor_tensor(SWB, bank(1, 0, NT * E).rearrange("p (i e) -> p i e", i=NT),
                                             over_tiles(BASE), ALU.add))
                link(nc.vector.tensor_tensor(CNT[:], CNT[:], bank(1, NT * E, (NT + 1) * E), ALU.add))
                linked()
                link(nc.vector.tensor_tensor(SWB, SWB, SEL, ALU.mult))
                settle()
                for i in range(NT):
                    link(nc.vector.max(V8[:, i, :], SWB[:, i, :]))
                linked()
                link(nc.vector.tensor_copy(SLOT1[:, bass.ds(b * NT, NT), 0:K], V8[:]))
                nc.vector.tensor_scalar(IDXB[:], V8[:], -1.0, None, ALU.add).then_inc(s_ix.sem, 1)
                for i in range(NT):
                    linked()
                    link(nc.vector.tensor_tensor(EQ, SWB[:, i, :].unsqueeze(1).to_broadcast([P, K, E]),
                                                 V8[:, i, :].unsqueeze(2).to_broadcast([P, K, E]), ALU.is_equal))
                    linked()
                    link(nc.vector.tensor_tensor(EQ, EQ, SCR[:, i, :].unsqueeze(1).to_broadcast([P, K, E]), ALU.mult))
                    linked()
                    link(nc.vector.tensor_reduce(WTS[:, b * NT + i, :], EQ, AX.X, ALU.add))
                dve.wait_ge(s_sg.sem, s_sg.value(b, 1))
                nc.vector.tensor_tensor(s_hid, s_gate, bank(3), ALU.mult).then_inc(s_sh.sem, 1)
                dve.wait_ge(s_sd.sem, s_sd.value(b, 1))
                for i in range(NT):
                    link(nc.vector.tensor_tensor(x_row(i), x_row(i),
                                                 bank(6 + i // 2, (i % 2) * D, (i % 2) * D + D), ALU.add))
                linked()
                nc.vector.sem_inc(s_dve.sem, s_dve.per_batch - n_links[0])
                nc.vector.sem_inc(s_batch, 1)

            steps = [0]

            def then(ins):
                ins.then_inc(s_tabc, 1)
                steps[0] += 1
                dve.wait_ge(s_tabc, steps[0])

            then(nc.vector.tensor_scalar(TI, CNT[:], float(P - 1), None, ALU.add))
            then(nc.vector.tensor_scalar(TI, TI, 7, None, ALU.logical_shift_right))
            then(nc.vector.tensor_copy(TF, TI))
            then(nc.vector.memset(ZERO, 0.0))
            then(nc.vector.memset(SLOT1[:, :, K:PARTS * PK], 1.0))
            then(nc.vector.memset(IND[:, 0, :], 1.0))
            then(nc.vector.tensor_tensor_scan(CUM, IND[:, 0, :], TF, 0.0, ALU.mult, ALU.add))
            then(nc.vector.tensor_scalar(NEED, CUM, 1.0, None, ALU.add))
            then(nc.vector.tensor_copy(COUNT_I, CNT[:]))
            for h in range(2):
                then(nc.vector.tensor_scalar(IND[:, h, :], CUM, tile_no[:, h:h + 1], None, ALU.is_le))
                then(nc.vector.tensor_reduce(TE[:, h:h + 1], IND[:, h, :], AX.X, ALU.add))
                then(nc.vector.tensor_tensor(IND[:, h, :], IND[:, h, :], TF, ALU.mult))
                then(nc.vector.tensor_reduce(TX[:, h:h + 1], IND[:, h, :], AX.X, ALU.add))
            then(nc.vector.tensor_tensor(TX[:], tile_no[:], TX[:], ALU.subtract))
            then(nc.vector.tensor_scalar(TX[:], TX[:], float(P), None, ALU.mult))
            then(nc.vector.scalar_tensor_tensor(TBF[:, :, 1], TE[:], float(REGION), TX[:], ALU.mult, ALU.add))
            then(nc.vector.tensor_scalar(TBF[:, :, 0], TBF[:, :, 1], float(E * REGION), None, ALU.min))
            then(nc.vector.tensor_scalar(TBF[:, :, 2], TE[:], float(E - 1), None, ALU.min))
            then(nc.vector.tensor_scalar(TBF[:, :, 3], TBF[:, :, 2], 1.0, None, ALU.add))
            then(nc.vector.memset(DD[:, 0:1], 0.0))
            then(nc.vector.tensor_scalar(DD[:, 1:E], TF[:, 0:E - 1], float(P), float(-REGION), ALU.mult, ALU.add))
            then(nc.vector.tensor_copy(TB[:], TBF[:]))
            then(nc.vector.tensor_scalar(TB[:, :, 2], TB[:, :, 2], RING - 1, None, ALU.bitwise_and))
            nc.vector.sem_inc(s_tab, 1)

            def tile_t(t, u):
                dve.wait_ge(e_T, t + 1)
                nc.vector.tensor_copy(XT[u % SLOTS], bank(u % 2, 0, D)).then_inc(e_XT, 1)

            def hidden(t, u):
                dve.wait_ge(e_SG, t + 1)
                nc.vector.tensor_tensor(HH[u % 2], SG[u % 2], bank(2 + u % 2, F, 2 * F), ALU.mult).then_inc(e_H, 1)

            for t in range(4):
                tile_t(t, t)
            for t in range(2):
                hidden(t, t)

            def dve_tile(t, u):
                tile_t(t + 4, u)
                hidden(t + 2, u)

            for part in range(PARTS):
                cols = slice(part * PK, part * PK + PK)
                with dve.Fori(0, B * NT) as m:
                    t, step = m * SLOTS + part * B * NT * SLOTS, m * 4 + part * B * NT * 4
                    dve_tile(t, 0)
                    nc.vector.tensor_tensor(MOVE, SLOT1[:, m, cols].unsqueeze(2).to_broadcast([P, PK, E]),
                                            region1[:].unsqueeze(1).to_broadcast([P, PK, E]), ALU.is_ge).then_inc(s_idx, 1)
                    dve_tile(t + 1, 1)
                    dve.wait_ge(s_idx, step + 1)
                    nc.vector.tensor_tensor(MOVE, MOVE, DD.unsqueeze(1).to_broadcast([P, PK, E]), ALU.mult).then_inc(s_idx, 1)
                    dve_tile(t + 2, 2)
                    dve.wait_ge(s_idx, step + 2)
                    nc.vector.tensor_reduce(V8[:, 0, 0:PK], MOVE, AX.X, ALU.add).then_inc(s_idx, 1)
                    dve_tile(t + 3, 3)
                    dve.wait_ge(s_idx, step + 3)
                    nc.vector.scalar_tensor_tensor(IDX[:, m, cols], SLOT1[:, m, cols], -1.0, V8[:, 0, 0:PK],
                                                   ALU.add, ALU.add).then_inc(s_idx, 1)
                    dve.wait_ge(s_idx, step + 4)

            with dve.Fori(0, B * NT) as t:
                for j in range(K):
                    dve.wait_ge(g_ld[j], t * 16 + 16)
                    dve.wait_ge(g_use, t * K + K + j)
                    last = nc.vector.scalar_tensor_tensor(X[:, t, :], G[j], WTS[:, t, j:j + 1], X[:, t, :],
                                                          ALU.mult, ALU.add).then_inc(g_use, 1)
                dve.wait_ge(g_use, t * K + 2 * K)
                nc.vector.sem_inc(s_fin, 1)

        @block.tensor
        def _(pe):
            pe.wait_ge(s_const, N_CONST)
            pe.wait_ge(ld_wqkv, 32)
            pe.wait_ge(ld_wo, 16)
            pe.wait_ge(ld_cross, CROSS_LOADS * 16)
            with pe.Fori(0, B) as b:
                pe.wait_ge(s_batch, b + 1)

                def transpose_rows(src, tiles, first_bank):
                    for c in range(DC):
                        for i in range(tiles):
                            at = (first_bank + c * (tiles // NT)) * BANK + i * P
                            last = nc.tensor.transpose(PS[:, at:at + P], src[:, i, c * P:(c + 1) * P], ident[:])
                    return last

                pe.wait_ge(s_xn.sem, s_xn.value(b, 1))
                transpose_rows(xn, NT, 5).then_inc(s_xnT.sem, 1)
                pe.wait_ge(s_xnTe.sem, s_xnTe.value(b, 1))
                for c in range(DC):
                    nc.tensor.matmul(bank(7), wkv[:, c, 0:HD], xnT[:, c, :], start=(c == 0), stop=(c == DC - 1))
                for i in range(NT):
                    for c in range(DC):
                        last = nc.tensor.matmul(bank(1, i * P, i * P + P), xnT[:, c, i * P:(i + 1) * P],
                                                wkv[:, c, HD:2 * HD], start=(c == 0), stop=(c == DC - 1))
                last.then_inc(s_kv.sem, 1)

                def q_proj(h):
                    if h:
                        pe.wait_ge(s_qe.sem, s_qe.value(b, h))
                    for c in range(DC):
                        last = nc.tensor.matmul(bank(0), wq[:, c, h * HD:(h + 1) * HD], xnT[:, c, :],
                                                start=(c == 0), stop=(c == DC - 1))
                    last.then_inc(s_q.sem, 1)

                def scores(h):
                    pe.wait_ge(s_qe.sem, s_qe.value(b, h + 1))
                    if h == 0:
                        pe.wait_ge(s_kvd.sem, s_kvd.value(b, 1))
                    else:
                        pe.wait_ge(s_exp.sem, s_exp.value(b, h))
                    for i in range(NT):
                        nc.tensor.matmul(S_PS[i], QT[h % 2][:, i * P:(i + 1) * P], KT[:, 0:P * (i + 1)],
                                         start=True, stop=False)
                        last = nc.tensor.matmul(S_PS[i][:, P * i:P * (i + 1)], ident16[:], causal16[:],
                                                start=False, stop=True)
                    last.then_inc(s_s.sem, 1)

                def transposes(h):
                    pe.wait_ge(s_norm.sem, s_norm.value(b, h + 1))
                    if h:
                        pe.wait_ge(s_ptd.sem, s_ptd.value(b, h))
                        pe.wait_ge(s_pta.sem, s_pta.value(b, h))
                    else:
                        pe.wait_ge(s_kva.sem, s_kva.value(b, 1))
                    for j in range(NT):
                        for i in range(j, NT):
                            last = nc.tensor.transpose(T_PS[j][:, P * (i - j):P * (i - j + 1)],
                                                       PR[h % 2][:, P_AT[i] + P * j:P_AT[i] + P * (j + 1)], ident[:])
                    last.then_inc(s_t.sem, 1)

                def attn(h):
                    pe.wait_ge(s_ptd.sem, s_ptd.value(b, h + 1))
                    pe.wait_ge(s_pta.sem, s_pta.value(b, h + 1))
                    if h:
                        pe.wait_ge(s_oe.sem, s_oe.value(b, h))
                    for j in range(NT):
                        last = nc.tensor.matmul(bank(7, P * j), V[:, j, :], PT[:, PT_AT[j]:PT_AT[j] + T - P * j],
                                                start=(j == 0), stop=(j == NT - 1))
                    last.then_inc(s_pv.sem, 1)

                q_proj(0)
                for h in range(H):
                    scores(h)
                    if h:
                        transposes(h - 1)
                    if h + 1 < H:
                        q_proj(h + 1)
                    if h:
                        attn(h - 1)
                transposes(H - 1)
                attn(H - 1)
                pe.wait_ge(s_oe.sem, s_oe.value(b, H))
                for i in range(NT):
                    for h in range(H):
                        last = nc.tensor.matmul(bank(2 + i // 2, (i % 2) * D, (i % 2) * D + D),
                                                OT[:, h, i * P:(i + 1) * P], wo[:, h, :],
                                                start=(h == 0), stop=(h == H - 1))
                last.then_inc(s_wo.sem, 1)

                pe.wait_ge(s_cn.sem, s_cn.value(b, 1))
                pe.wait_ge(s_xn.sem, s_xn.value(b, 2))
                transpose_rows(C, SC, 0).then_inc(s_cT.sem, 1)
                transpose_rows(xn, NT, 4).then_inc(s_xnT.sem, 1)
                pe.wait_ge(s_cTe.sem, s_cTe.value(b, 1))
                for n in range(SC):
                    for c in range(DC):
                        last = nc.tensor.matmul(bank(n // 2, (n % 2) * D, (n % 2) * D + D), CT[:, c, n * P:(n + 1) * P],
                                                xwv[:, c, :], start=(c == 0), stop=(c == DC - 1))
                last.then_inc(s_vx.sem, 1)
                pe.wait_ge(s_xnTe.sem, s_xnTe.value(b, 2))
                def project(g):
                    for half in range(2):
                        for c in range(DC):
                            last = nc.tensor.matmul(bank(half), wk_g[:, c, g, :], CT[:, c, half * T:(half + 1) * T],
                                                    start=(c == 0), stop=(c == DC - 1))
                        last.then_inc(s_pk[half].sem, 1)
                    for c in range(DC):
                        last = nc.tensor.matmul(bank(7), wq_g[:, c, g, :], xnT[:, c, :],
                                                start=(c == 0), stop=(c == DC - 1))
                    last.then_inc(s_pq.sem, 1)

                def max_scores(g, n):
                    j, i, half = n // (2 * NT), n // 2 % NT, n % 2
                    k = g * 2 * NT * HG + n
                    if n % (2 * NT) == 0:
                        st = s_stack[g % 2][j]
                        pe.wait_ge(st.sem, st.value(b, g // 2 + 1))
                    if n < 2:
                        pe.wait_ge(s_lo.sem, s_lo.value(b, 3 * min(g + 1, NG) if g else 3))
                    if k >= 2:
                        pe.wait_ge(s_p1d.sem, s_p1d.value(b, k - 1))
                    nc.tensor.matmul(bank(k % 2), QS[g % 2][:, j, i * P:(i + 1) * P],
                                     KS[g % 2][:, j, half * T:(half + 1) * T], start=True, stop=True).then_inc(s_p1.sem, 1)

                def gap(g):
                    pe.wait_ge(s_mx.sem, s_mx.value(b, g + 1))
                    if g:
                        pe.wait_ge(s_ex.sem, s_ex.value(b, g * 2 * SC))
                    for i in range(NT):
                        last = nc.tensor.transpose(bank(2, i * P, i * P + P), MX[:, i].rearrange("p j w -> p (j w)"), ident[:])
                    last.then_inc(s_mT.sem, 1)
                    if g + 1 < NG:
                        if g:
                            pe.wait_ge(s_lo.sem, s_lo.value(b, 3 * g + 3))
                        pe.wait_ge(s_qr.sem, s_qr.value(b, g + 1))
                        project(g + 1)
                def cross_scores(g, u):
                    c, n = u // 2, g * 2 * SC + u
                    if u < 2:
                        pe.wait_ge(s_ml.sem, s_ml.value(b, g + 1))
                        pe.wait_ge(s_aug.sem, s_aug.value(b, g + 1))
                    else:
                        pe.wait_ge(s_ex.sem, s_ex.value(b, n - 1))
                    for jj in range(2):
                        j = 2 * (u % 2) + jj
                        last = nc.tensor.matmul(bank(2 + 2 * (u % 2) + jj), KS[g % 2][:, j, c * P:(c + 1) * P],
                                                QS[g % 2][:, j, :], start=True, stop=True)
                    last.then_inc(s_st.sem, 1)

                def cross_pv(g, u):
                    c, n = u // 2, g * 2 * SC + u
                    pe.wait_ge(s_ex.sem, s_ex.value(b, n + 1))
                    if u < 2 and g:
                        pe.wait_ge(s_or.sem, s_or.value(b, g))
                    for jj in range(2):
                        j = 2 * (u % 2) + jj
                        last = nc.tensor.matmul(PS[W * j:W * j + XE + 1, 6 * BANK:7 * BANK], VX[:, c, HG * g + j, :],
                                                PX[u % 2][:, jj, :], start=(c == 0), stop=(c == SC - 1))
                    last.then_inc(s_pvx.sem, 1)

                pe.wait_ge(s_vxe.sem, s_vxe.value(b, 1))
                project(0)
                for n in range(2 * NT * HG):
                    max_scores(0, n)
                for g in range(NG):
                    gap(g)
                    cross_scores(g, 0)
                    cross_scores(g, 1)
                    done = 0
                    for u in range(2 * SC):
                        cross_pv(g, u)
                        if u + 2 < 2 * SC:
                            cross_scores(g, u + 2)
                        if g + 1 < NG and u >= FIRST_MAX_UNIT:
                            upto = 2 * NT * HG * (u - FIRST_MAX_UNIT + 1) // (2 * SC - FIRST_MAX_UNIT)
                            for n in range(done, upto):
                                max_scores(g + 1, n)
                            done = upto
                pe.wait_ge(s_xn.sem, s_xn.value(b, 3))
                transpose_rows(xn, NT, 4).then_inc(s_xnT.sem, 1)
                pe.wait_ge(s_xnTe.sem, s_xnTe.value(b, 3))
                for i in range(NT):
                    for c in range(DC):
                        last = nc.tensor.matmul(bank(2 + i // 2, (i % 2) * D, (i % 2) * D + D),
                                                xnT[:, c, i * P:(i + 1) * P], xwo[:, c, :],
                                                start=(c == 0), stop=(c == DC - 1))
                last.then_inc(s_xo.sem, 1)

                pe.wait_ge(s_xn.sem, s_xn.value(b, 4))
                transpose_rows(xr, NT, 4).then_inc(s_xnT.sem, 1)
                pe.wait_ge(s_xnTe.sem, s_xnTe.value(b, 4))
                for i in range(NT):
                    for c in range(DC):
                        last = nc.tensor.matmul(bank(0, i * E, (i + 1) * E), xnT[:, c, i * P:(i + 1) * P], wr[:, c, :],
                                                start=(c == 0), stop=(c == DC - 1))
                last.then_inc(s_lg.sem, 1)
                for n in range(2):
                    for c in range(DC):
                        last = nc.tensor.matmul(bank(2 + n), ws_gu[:, c, n * F:(n + 1) * F], xnT[:, c, :],
                                                start=(c == 0), stop=(c == DC - 1))
                last.then_inc(s_gu.sem, 1)
                pe.wait_ge(s_sel.sem, s_sel.value(b, 1))
                for i in range(NT):
                    for k in range(i + 1):
                        nc.tensor.matmul(bank(1, i * E, (i + 1) * E), before16[:] if k == i else ones16[:],
                                         SEL16[:, k, :], start=(k == 0), stop=(k == i))
                for k in range(NT):
                    last = nc.tensor.matmul(bank(1, NT * E, (NT + 1) * E), ones16[:], SEL16[:, k, :],
                                            start=(k == 0), stop=(k == NT - 1))
                last.then_inc(s_rk.sem, 1)
                pe.wait_ge(s_sh.sem, s_sh.value(b, 1))
                for i in range(NT):
                    last = nc.tensor.matmul(bank(6 + i // 2, (i % 2) * D, (i % 2) * D + D),
                                            s_hid[:, i * P:(i + 1) * P], ws_d[:], start=True, stop=True)
                last.then_inc(s_sd.sem, 1)

            pe.wait_ge(s_batch, B + 1)
            pe.wait_ge(s_tabl, 16)
            nc.tensor.sem_inc(e_D, 1)

            def transposes_of(slot, bank_no, loaded):
                pe.wait_ge(e_ld[slot], loaded)
                for c in range(DC):
                    last = nc.tensor.transpose(bank(bank_no, c * P, (c + 1) * P), XS[slot][:, c * P:(c + 1) * P], ident[:])
                last.then_inc(e_T, 1)

            def ring_slot(t):
                return pe.value_load(TROW[0:1, bass.ds(t * FIELDS + 2, 1)], min_val=0, max_val=RING - 1)

            def gate_up(slot, u):
                for c in range(DC):
                    last = nc.tensor.matmul(bank(2 + u % 2, 0, 2 * F), XT[u % SLOTS][:, c * P:(c + 1) * P],
                                            w_ring[:, bass.ds(slot, 1), c * 2 * F:(c + 1) * 2 * F].squeeze(1),
                                            start=(c == 0), stop=(c == DC - 1))
                last.then_inc(e_GU, 1)

            def hidden_rows_t(t, u):
                pe.wait_ge(e_H, t + 1)
                nc.tensor.transpose(bank(4 + u % 2, 0, P), HH[u % 2], ident[:]).then_inc(e_HP, 1)

            for t in range(4):
                if t >= 2:
                    pe.wait_ge(e_XT, t - 1)
                transposes_of(t, t % 2, 16)
            for t in range(2):
                slot = ring_slot(t)
                pe.wait_ge(e_XT, t + 1)
                gate_up(slot, t)
            hidden_rows_t(0, 0)
            with pe.Fori(0, TILES // LOADED) as n:
                for u in range(LOADED):
                    t = n * LOADED + u
                    slot = ring_slot(t + 2)
                    pe.wait_ge(e_XT, t + 3)
                    pe.wait_ge(e_H, t + 1)
                    gate_up(slot, u + 2)
                    transposes_of((u + 4) % LOADED, u % 2, n * 16 + 16 * ((u + 4) // LOADED + 1))
                    hidden_rows_t(t + 1, u + 1)
                    slot = ring_slot(t)
                    pe.wait_ge(e_HT, t + 1)
                    pe.wait_ge(e_O, t + 1)
                    nc.tensor.matmul(bank(6 + u % 2, 0, D), HT[u % 2], w_ring[:, bass.ds(slot, 1), 4 * F:4 * F + D].squeeze(1),
                                     start=True, stop=True).then_inc(e_D, 1)


NAMES = ['x', 'ctx_1024', 'L0_attn_Wq', 'L0_attn_bq', 'L0_attn_Wkv', 'L0_attn_bkv', 'L0_attn_Wo',
         'L0_xattn_norm_w', 'L0_xattn_norm_b', 'L0_xattn_norm1_w', 'L0_xattn_norm1_b', 'L0_xattn_Wq',
         'L0_xattn_bq', 'L0_xattn_Wk', 'L0_xattn_bk', 'L0_xattn_Wv', 'L0_xattn_bv', 'L0_xattn_Wo',
         'L0_xattn_bo', 'L0_ffn_w_router', 'L0_ffn_b_router', 'L0_ffn_we_gate', 'L0_ffn_we_up',
         'L0_ffn_we_down', 'L0_ffn_ws_gate', 'L0_ffn_ws_up', 'L0_ffn_ws_down']


def kernel(**inputs):
    import numpy as np
    import concourse.bacc as bacc
    from concourse.bass_utils import run_bass_kernel_spmd

    nc = bacc.Bacc("TRN2", target_bir_lowering=False, num_devices=1)
    arrays = {n: np.ascontiguousarray(inputs[n]) for n in NAMES}
    freq = np.exp(np.float32(-np.log(10000.0)) * np.arange(0, HD, 2, dtype=np.float32) / np.float32(HD))
    angle = np.arange(T, dtype=np.float32)[None, :] * freq.astype(np.float32)[:, None]
    table = np.empty((HD, T), np.float32)
    table[0::2] = np.sin(angle)
    table[1::2] = np.cos(angle)
    arrays["position_t"] = table
    aps = {n: nc.dram_tensor("in_" + n, v.shape, F32, kind="ExternalInput").ap() for n, v in arrays.items()}
    out = nc.dram_tensor("out", (B, T, D), F32, kind="ExternalOutput").ap()
    build(nc, aps, out)
    r = run_bass_kernel_spmd(nc, [{"in_" + n: v for n, v in arrays.items()}], core_ids=[0])
    return r.results[0]["out"]
```

```python
import concourse.bass as bass
from concourse import mybir
from contextlib import ExitStack

F32 = mybir.dt.float32
F32R = mybir.dt.float32r
BF16 = mybir.dt.bfloat16
I32 = mybir.dt.int32
U32 = mybir.dt.uint32
ALU = mybir.AluOpType
ACT = mybir.ActivationFunctionType
AX = mybir.AxisListType

P = 128
B, T, D = 4, 512, 256
NT, DC = T // P, D // P
H, HD = 8, 128
S, XH, XE = 1024, 16, 16
SC = S // P
HG, NG = 4, 4
W = P // HG
E, F, K = 64, 128, 8
GR = 8
EPS = 1e-5
SELF_SCALE = float(HD) ** -0.5
CROSS_SCALE = float(XE) ** -0.5
ROUTED = 2.5
NEG = -1e30
REGION = B * T + P
TILES = B * T * K // P + E
P_AT = [P * i * (i + 1) // 2 for i in range(NT)]
PT_AT = [0, 512, 896, 1152]
TRI = P * NT * (NT + 1) // 2
BANK = 512
NORMS = 5
BLOCKS = 4
RING = 8
SLOTS = 4
LOADED = 8
FIELDS = 4
ROWS_IN = E * REGION + P
ROWS_OUT = TILES * P
FFN_LOADS = 5
CROSS_LOADS = 8 + 2 * DC + 3 * HG
MAX_UNITS = 10
PARTS = TILES // (4 * B * 4)
PK = -(-K // PARTS)
HALF = K // 2
N_CONST = 8


class Signal:

    def __init__(self, sem, per_batch, step=1):
        self.sem, self.per_batch, self.step = sem, per_batch, step

    def value(self, b, k):
        return b * (self.per_batch * self.step) + k * self.step


def build(nc, a, out):
    ctx = ExitStack()
    with ctx:
        def sb(name, shape, dt=F32):
            return ctx.enter_context(nc.sbuf_tensor(name, shape, dt))

        def sem(name):
            return ctx.enter_context(nc.semaphore(name))

        def signal(name, per_batch, step=1):
            return Signal(sem(name), per_batch, step)

        X = sb("residual", [P, B * NT, D])
        attn_space = sb("attn_space", [P, H * T + DC * H * HD + H * D])
        wide = attn_space[:, 0:H * T]
        wq = attn_space[:, H * T:H * T + DC * H * HD].rearrange("p (c n) -> p c n", c=DC)
        wkv = sb("self_wkv", [P, DC, 2 * HD])
        wo = attn_space[:, H * T + DC * H * HD:].rearrange("p (h d) -> p h d", h=H)
        bq = sb("self_bq", [P, H])
        bkv = sb("self_bkv", [P, 2])
        peT = sb("position_t", [P, T])
        ident = sb("identity", [P, P])
        ident16 = sb("identity16", [P, P], BF16)
        causal16 = sb("causal16", [P, P], BF16)
        stats = sb("ln_stats", [P, SC, 6])
        mv = sb("ln_mean_var", [P, SC, 2])
        vep = sb("ln_var_eps", [P, SC])
        rstd = sb("ln_rstd", [P, SC])
        mhalf = sb("minus_half", [P, SC])
        scratch = sb("scratch", [P, 1])
        pool_scratch = sb("pool_scratch", [P, 1])
        carry = sb("pool_carry", [P, 2 * NT])
        pool_scratch2 = sb("pool_scratch2", [P, 1])
        C = sb("context", [P, SC, D])
        c_stats = sb("context_stats", [P, SC, 6])
        c_mv = sb("context_mean_var", [P, SC, 2])
        c_vep = sb("context_var_eps", [P, SC])
        c_rstd = sb("context_rstd", [P, SC])
        xwv = sb("cross_wv", [P, DC, D])
        xwo = sb("cross_wo", [P, DC, D])
        wq_g = sb("cross_wq_group", [P, DC, NG, P])
        wk_g = sb("cross_wk_group", [P, DC, NG, P])
        bq_g = sb("cross_bq_group", [P, NG])
        bk_g = sb("cross_bk_group", [P, NG])
        ones4 = sb("ones4", [HG, NG])
        norm_w = sb("norm_w", [P, DC])
        norm_b = sb("norm_b", [P, DC])
        norm1_w = sb("norm1_w", [P, DC])
        norm1_b = sb("norm1_b", [P, DC])
        bv_row = sb("cross_bv_row", [P, D])
        bo_row = sb("cross_bo_row", [P, D])
        VX = sb("cross_v", [P, SC, XH, XE + 1])
        k_hi = sb("k_hi", [P, S], F32R)
        k_lo = sb("k_lo", [P, S], F32R)
        q_hi = sb("q_hi", [P, T], F32R)
        q_lo = sb("q_lo", [P, T], F32R)
        m_hi = sb("max_hi", [P, T], F32R)
        m_lo = sb("max_lo", [P, T], F32R)
        QM = sb("q_apart", [P, HG, T], F32R)
        KS = [sb(f"k_stack{i}", [P, HG, S], F32R) for i in range(2)]
        QS = [sb(f"q_stack{i}", [P, HG, T], F32R) for i in range(2)]
        MP = sb("max_halves", [P, 2, NT, HG])
        MX = sb("max_columns", [P, NT, HG, W])
        PT = sb("probs_t", [P, TRI])
        PX = [sb("cross_probs0", [P, 2, T]), PT[:, 0:2 * T].rearrange("p (j t) -> p j t", j=2)]
        q_whole = sb("q_whole", [P, T])
        QT = [sb(f"q_t{i}", [P, T]) for i in range(2)]
        QR = [QT[i][:].rearrange("p (m w) -> p m w", w=W) for i in range(2)]
        OR = sb("out_rows", [P, XE, W])
        RG = sb("cross_row_inv", [P, XE])
        xn = sb("normed", [P, NT, D])
        xnT = sb("normed_t", [P, DC, T])
        KT = sb("k_t", [P, T])
        V = sb("v", [P, NT, HD])
        PR = [sb(f"probs{i}", [P, TRI]) for i in range(2)]
        OT = wide.rearrange("p (h t) -> p h t", h=H)
        CT = wide[:, 0:DC * S].rearrange("p (c s) -> p c s", c=DC)
        O = wide[:, DC * S:DC * S + NT * D].rearrange("p (i d) -> p i d", i=NT)
        mx = sb("row_max", [P, NT])
        nb = sb("exp_bias", [P, NT])
        rsum = sb("row_sum", [P, NT])
        rinv = sb("row_inv", [P, NT])

        wr = sb("router_w", [P, DC, E])
        br_row = sb("router_b_row", [P, E])
        ws_gu = sb("shared_gate_up", [P, DC, 2 * F])
        ws_d = sb("shared_down", [P, D])
        before16 = sb("before16", [P, P], BF16)
        ones16 = sb("ones16", [P, P], BF16)
        lower8 = sb("lower8", [P, GR, GR])
        region_i = PT[:, 0:E].bitcast(I32)
        region1 = sb("region1", [P, E])
        tile_i = sb("tile_i", [P, 2], I32)
        tile_no = sb("tile_no", [P, 2])
        xr = PX[0][:].rearrange("p a t -> p (a t)").rearrange("p (i d) -> p i d", d=D)
        def in_probs(which, n, inner):
            return PR[which][:, n * NT * E:(n + 1) * NT * E].rearrange(inner, i=NT, g=GR)

        SCR = in_probs(0, 0, "p (i g e) -> p i (g e)")
        SWB = in_probs(0, 1, "p (i g e) -> p i (g e)")
        SRT = in_probs(0, 2, "p (i g e) -> p i g e")
        CMP = in_probs(0, 3, "p (i g e) -> p i g e")
        CMQ = in_probs(0, 4, "p (i g e) -> p i g e")
        SEL = in_probs(1, 0, "p (i g e) -> p i (g e)")
        GS = sb("group_scores", [P, NT, GR])
        TOP = sb("top_scores", [P, NT, K])
        SEL16 = sb("selected16", [P, NT, E], BF16)
        WSUM = sb("weight_sum", [P, NT])
        CNT = sb("expert_counts", [P, E])
        def beside(col, n):
            return PR[1][:, NT * E + col:NT * E + col + n]

        BASE = beside(7 * E, E)
        V8 = sb("slots_sorted", [P, NT, K])
        IDXB = sb("batch_slots", [P, NT, K], U32)
        SLOT1 = sb("token_slots_1", [P, B * NT, PARTS * PK])
        IDX = sb("token_results", [P, B * NT, PARTS * PK], U32)
        WTS = sb("token_weights", [P, B * NT, K])
        ZERO = beside(8 * E, D)
        MOVE = beside(8 * E + D, PK * E).rearrange("p (j e) -> p j e", e=E)
        TF = beside(2 * E, E)
        TI = beside(3 * E, E).bitcast(I32)
        CUM = beside(4 * E, E)
        NEED = beside(5 * E, E).bitcast(I32)
        DD = BASE
        COUNT_I = beside(6 * E, E).bitcast(I32)
        IND = beside(0, 2 * E).rearrange("p (h e) -> p h e", h=2)
        TE = sb("tile_expert", [P, 2])
        TX = sb("tile_excess", [P, 2])
        TBF = sb("tile_fields_f", [P, 2, FIELDS])
        TB = sb("tile_fields", [P, 2, FIELDS], I32)
        TROW = PT[0:1, 0:2 * P * FIELDS].bitcast(I32)
        w_ring = attn_space[:, 0:RING * 3 * D].rearrange("p (s n) -> p s n", s=RING)
        SG = [attn_space[:, 6656 + i * F:6656 + (i + 1) * F] for i in range(2)]
        HH = [attn_space[:, 6912 + i * F:6912 + (i + 1) * F] for i in range(2)]
        HT = [attn_space[:, 7168 + i * P:7168 + (i + 1) * P] for i in range(2)]
        XS = [C[:, i, :] for i in range(LOADED)]
        XT = [xn[:, i, :] for i in range(SLOTS)]
        OS = [QR[i // 2][:].rearrange("p m w -> p (m w)")[:, (i % 2) * D:(i % 2 + 1) * D] for i in range(SLOTS)]
        OS2 = [QR[i][:].rearrange("p m w -> p (m w)").rearrange("p (i d) -> p i d", d=D) for i in range(2)]
        G = [C[:, j, :] for j in range(K)]
        EQ = QR[0][:].rearrange("p m w -> p (m w)").rearrange("p (j e) -> p j e", e=E)
        s_gate = q_whole[:]
        s_hid = OR[:].rearrange("p m w -> p (m w)")

        rows_in = nc.dram_tensor("rows_in", (ROWS_IN, D), F32, kind="Internal").ap()
        rows_out = nc.dram_tensor("rows_out", (ROWS_OUT, D), F32, kind="Internal").ap()
        table = nc.dram_tensor("tile_rows", (2 * P, FIELDS), I32, kind="Internal").ap()

        PS = ctx.enter_context(nc.psum_tensor("psum", [P, 8 * BANK], F32))

        def bank(n, lo=0, hi=BANK):
            return PS[:, n * BANK + lo:n * BANK + hi]

        def max_banks(g):
            return 6 if g == 0 else 3

        def max_bank(g, n):
            return n % 6 if g == 0 else (0, 1, 7)[n % 3]

        S_PS = [bank(3, 384, 512), bank(4, 0, 256), bank(3, 0, 384), bank(2)]
        T_PS = [bank(5), bank(6, 0, 384), bank(1, 0, 256), bank(6, 384, 512)]

        ld_x = [sem(f"x_loaded{i}") for i in range(B)]
        ld_small = sem("small_loaded")
        ld_wqkv = sem("wqkv_loaded")
        ld_wo = sem("wo_loaded")
        s_const = sem("constants_made")
        s_const0 = sem("constants_cleared")
        s_batch = sem("batch_done")
        ld_ctx = signal("context_loaded", 1, 16)
        ld_cross = sem("cross_loaded")
        s_pad = sem("padded_cleared")
        s_vones = sem("ones_columns_set")
        s_cvar = signal("context_variance", 1)
        s_crstd = signal("context_rstd_ready", 1)
        s_cn = signal("context_normed", 1)
        s_cT = signal("context_transposed", 1)
        s_cTe = signal("context_t_ready", 1)
        s_vx = signal("cross_v_projected", 1)
        s_vxe = signal("cross_v_ready", 1)
        s_qw = signal("q_whole_ready", NG)
        s_qr = signal("q_rows_ready", NG)
        s_pk = [signal(f"group_k{i}_projected", NG) for i in range(2)]
        s_pq = signal("group_q_projected", NG)
        s_hi = signal("high_parts_ready", 3 * NG)
        s_lo = signal("low_parts_ready", 3 * NG)
        s_stack = [[signal(f"stack{i}_head{j}", NG // 2, 8 * 16) for j in range(HG)] for i in range(2)]
        s_qm0 = sem("q_apart_cleared")
        s_qm = signal("q_apart_ready", NG)
        s_p1 = signal("max_scores_ready", NG * NT * HG * 2)
        s_p1d = signal("max_scores_taken", NG * NT * HG * 2)
        s_mx = signal("max_ready", NG)
        s_mT = signal("max_transposed", NG)
        s_mh = signal("max_high_ready", NG)
        s_ml = signal("max_low_ready", NG)
        s_aug = signal("max_rows_stacked", NG, 8 * 16)
        s_st = signal("cross_scores_ready", NG * SC * 2)
        s_ex = signal("cross_exp_done", NG * SC * 2)
        s_pvx = signal("cross_pv_done", NG * SC * 2)
        s_or = signal("out_rows_taken", NG)
        s_o = signal("cross_out_ready", NG)
        s_xo = signal("cross_wo_projected", 1)
        s_out = sem("stored")
        s_dve = signal("dve_step", 1000)
        s_var = signal("variance_ready", NORMS)
        s_rstd = signal("rstd_ready", NORMS)
        s_xn = signal("normed_ready", BLOCKS)
        s_xnT = signal("normed_transposed", BLOCKS)
        s_xnTe = signal("normed_t_ready", BLOCKS)
        s_kv = signal("kv_projected", 1)
        s_kvd = signal("k_t_ready", 1)
        s_kva = signal("v_ready", 1)
        s_q = signal("q_projected", H)
        s_qe = signal("q_t_ready", H)
        s_s = signal("scores_ready", H)
        s_nb = signal("exp_bias_ready", H)
        s_exp = signal("exp_done", H)
        s_norm = signal("probs_ready", H)
        s_t = signal("probs_transposed", H)
        s_ptd = signal("probs_t_dve", H)
        s_pta = signal("probs_t_act", H)
        s_pv = signal("attn_ready", H)
        s_oe = signal("attn_t_ready", H)
        s_wo = signal("wo_projected", 1)

        ld_ffn = sem("ffn_loaded")
        s_zero = sem("zero_rows_ready")
        s_lg = signal("logits_ready", 1)
        s_gu = signal("shared_gate_up_ready", 1)
        s_ez = signal("logits_exp_ready", 1)
        s_sg = signal("shared_silu_ready", 1)
        s_sh = signal("shared_hidden_ready", 1)
        s_sd = signal("shared_out_ready", 1)
        s_sel = signal("experts_selected", 1)
        s_rk = signal("ranks_ready", 1)
        s_ix = signal("slots_ready", 1)
        s_scat = signal("rows_scattered", NT * K, 16)
        e_ld = [sem(f"tile_loaded{i}") for i in range(LOADED)]
        e_st = [sem(f"tiles_stored{i}") for i in range(2)]
        e_T = sem("tile_transposed")
        e_XT = sem("tile_t_ready")
        e_GU = sem("gate_up_ready")
        e_SG = sem("silu_ready")
        e_H = sem("hidden_ready")
        e_HP = sem("hidden_transposed")
        e_HT = sem("hidden_t_ready")
        e_may = sem("tile_may_load")
        e_D = sem("down_ready")
        e_O = sem("tile_out_ready")
        w_dma = [sem(f"weights_landing{i}") for i in range(2)]
        w_ready = sem("weights_ready")
        s_tab = sem("table_made")
        s_tabc = sem("table_step")
        s_idx = sem("result_row_step")
        s_tabd = sem("table_stored")
        s_tabl = sem("table_loaded")
        s_copied = sem("result_rows_copied")
        g_ld = [sem(f"result_gathered{j}") for j in range(K)]
        g_use = sem("results_added")
        s_fin = sem("rows_finished")

        block = ctx.enter_context(nc.Block())

        @block.sync
        def _(sp):
            xv = a["x"].rearrange("b (i p) d -> b p i d", p=P)
            sp.dma_start(X[:, 0:NT, :], xv[0]).then_inc(ld_x[0], 16)
            sp.dma_start(wkv[:], a["L0_attn_Wkv"].rearrange("(c p) n -> p c n", p=P)).then_inc(ld_wqkv, 16)
            sp.dma_start(wq, a["L0_attn_Wq"].rearrange("(c p) n -> p c n", p=P)).then_inc(ld_wqkv, 16)
            sp.dma_start(peT[:], a["position_t"]).then_inc(ld_small, 16)
            sp.dma_start(bq[:], a["L0_attn_bq"].rearrange("(h p) -> p h", p=P), allow_slow_non_contiguous=True).then_inc(ld_small, 16)
            sp.dma_start(bkv[:], a["L0_attn_bkv"].rearrange("(h p) -> p h", p=P), allow_slow_non_contiguous=True).then_inc(ld_small, 16)
            sp.dma_start(wo, a["L0_attn_Wo"].rearrange("(h p) n -> p h n", p=P)).then_inc(ld_wo, 16)
            for i in range(1, B):
                sp.dma_start(X[:, i * NT:(i + 1) * NT, :], xv[i]).then_inc(ld_x[i], 16)

            def stack(b, g):
                sp.wait_ge(s_lo.sem, s_lo.value(b, 3 * g + 3))
                for j in range(HG):
                    done = s_stack[g % 2][j].sem
                    for t, (kp, qp) in enumerate(((k_hi, q_hi), (k_lo, q_hi), (k_hi, q_lo), (k_lo, q_lo))):
                        rows, head = slice(W * t, W * t + W), slice(W * j, W * j + W)
                        sp.dma_start(KS[g % 2][rows, j, :].bitcast(F32), kp[head, :].bitcast(F32)).then_inc(done, 16)
                        sp.dma_start(QS[g % 2][rows, j, :].bitcast(F32), qp[head, :].bitcast(F32)).then_inc(done, 16)

            def stack_max(b, g):
                sp.wait_ge(s_mh.sem, s_mh.value(b, g + 1))
                for j in range(HG):
                    sp.dma_start(QS[g % 2][XE:XE + 1, j, :].bitcast(F32),
                                 m_hi[W * j + XE:W * j + XE + 1, :].bitcast(F32)).then_inc(s_aug.sem, 16)
                sp.wait_ge(s_ml.sem, s_ml.value(b, g + 1))
                for j in range(HG):
                    sp.dma_start(QS[g % 2][2 * W + XE:2 * W + XE + 1, j, :].bitcast(F32),
                                 m_lo[W * j + XE:W * j + XE + 1, :].bitcast(F32)).then_inc(s_aug.sem, 16)

            sp.dma_start(norm_w[:], a["L0_xattn_norm_w"].rearrange("(c p) -> p c", p=P), allow_slow_non_contiguous=True).then_inc(ld_cross, 16)
            sp.dma_start(norm_b[:], a["L0_xattn_norm_b"].rearrange("(c p) -> p c", p=P), allow_slow_non_contiguous=True).then_inc(ld_cross, 16)
            sp.dma_start(norm1_w[:], a["L0_xattn_norm1_w"].rearrange("(c p) -> p c", p=P), allow_slow_non_contiguous=True).then_inc(ld_cross, 16)
            sp.dma_start(norm1_b[:], a["L0_xattn_norm1_b"].rearrange("(c p) -> p c", p=P), allow_slow_non_contiguous=True).then_inc(ld_cross, 16)
            sp.dma_start(bv_row[:], a["L0_xattn_bv"].partition_broadcast(P)).then_inc(ld_cross, 16)
            sp.dma_start(bo_row[:], a["L0_xattn_bo"].partition_broadcast(P)).then_inc(ld_cross, 16)
            sp.dma_start(xwv[:], a["L0_xattn_Wv"].rearrange("(c p) n -> p c n", p=P)).then_inc(ld_cross, 16)
            sp.dma_start(xwo[:], a["L0_xattn_Wo"].rearrange("(c p) n -> p c n", p=P)).then_inc(ld_cross, 16)
            sp.wait_ge(s_pad, 5)
            for c in range(DC):
                for w_g, w in ((wq_g, a["L0_xattn_Wq"]), (wk_g, a["L0_xattn_Wk"])):
                    sp.dma_start(w_g[:, c, :, :].rearrange("p g (j w) -> p (g j) w", j=HG)[:, :, 0:XE],
                                 w[c * P:(c + 1) * P, :].rearrange("p (h e) -> p h e", e=XE)).then_inc(ld_cross, 16)
            for j in range(HG):
                for b_g, v in ((bq_g, a["L0_xattn_bq"]), (bk_g, a["L0_xattn_bk"])):
                    sp.dma_start(b_g[W * j:W * j + XE, :], v.rearrange("(g j e) -> j e g", j=HG, e=XE)[j],
                                 allow_slow_non_contiguous=True).then_inc(ld_cross, 16)
                sp.dma_start(bk_g[W * j + XE:W * j + XE + 1, :], ones4[j:j + 1, :]).then_inc(ld_cross, 16)

            sp.dma_start(wr[:], a["L0_ffn_w_router"].rearrange("(c p) n -> p c n", p=P)).then_inc(ld_ffn, 16)
            sp.dma_start(br_row[:], a["L0_ffn_b_router"].partition_broadcast(P)).then_inc(ld_ffn, 16)
            sp.dma_start(ws_gu[:, :, 0:F], a["L0_ffn_ws_gate"].rearrange("(c p) n -> p c n", p=P)).then_inc(ld_ffn, 16)
            sp.dma_start(ws_gu[:, :, F:2 * F], a["L0_ffn_ws_up"].rearrange("(c p) n -> p c n", p=P)).then_inc(ld_ffn, 16)
            sp.dma_start(ws_d[:], a["L0_ffn_ws_down"]).then_inc(ld_ffn, 16)

            with sp.Fori(0, B) as b:
                stack(b, 0)
                for g in range(NG):
                    stack_max(b, g)
                    if g + 1 < NG:
                        stack(b, g + 1)

            gate, up, down = a["L0_ffn_we_gate"], a["L0_ffn_we_up"], a["L0_ffn_we_down"]

            def load_weights(e, slot):
                w = w_ring[:, slot, 0:4 * F].rearrange("p (c n) -> p c n", c=DC)
                sp.dma_start(w[:, :, 0:F], gate[e].rearrange("(c p) n -> p c n", p=P)).then_inc(w_dma[slot % 2], 16)
                sp.dma_start(w[:, :, F:2 * F], up[e].rearrange("(c p) n -> p c n", p=P)).then_inc(w_dma[slot % 2], 16)
                sp.dma_start(w_ring[:, slot, 4 * F:4 * F + D], down[e]).then_inc(w_dma[slot % 2], 16)

            def pad(e, slot):
                last_row = sp.value_load(COUNT_I[0:1, bass.ds(e, 1)], min_val=0, max_val=B * T)
                sp.dma_start(rows_in[bass.ds(e * REGION + last_row, P), :], ZERO).then_inc(w_dma[slot % 2], 16)

            sp.wait_ge(s_batch, B + 1)
            for e in range(RING):
                load_weights(e, e)
            sp.wait_ge(s_tab, 1)
            sp.dma_start(table.rearrange("(h p) f -> p h f", h=2), TB[:]).then_inc(s_tabd, 16)
            sp.wait_ge(s_tabd, 16)
            sp.dma_start(TROW, table.rearrange("(o t) f -> o (t f)", o=1)).then_inc(s_tabl, 16)
            sp.wait_ge(s_tabl, 16)
            sp.dma_start(rows_in[E * REGION:ROWS_IN, :], ZERO).then_inc(s_zero, 16)
            sp.wait_ge(s_scat.sem, s_scat.value(B, 1))
            for e in range(RING):
                pad(e, e)
            for i in range(2):
                sp.wait_ge(w_dma[i], 4 * 16 * RING // 2)
            nc.sync.sem_inc(w_ready, RING - 2)
            with sp.Fori(1, E // RING) as n:
                for u in range(RING):
                    need = sp.value_load(NEED[0:1, bass.ds(n * RING + u - RING, 1)], min_val=1, max_val=TILES + 1)
                    sp.wait_ge(w_dma[u % 2], n * (64 * RING // 2) + 64 * (u // 2))
                    nc.sync.sem_inc(w_ready, 1)
                    sp.wait_ge(e_D, need)
                    load_weights(n * RING + u, u)
                    pad(n * RING + u, u)
            for i in range(2):
                sp.wait_ge(w_dma[i], 4 * 16 * E // 2)
                nc.sync.sem_inc(w_ready, 1)

            ov = out.rearrange("b (i p) d -> (b i) p d", p=P)
            with sp.Fori(0, B * NT) as t:
                sp.wait_ge(s_fin, t + 1)
                sp.dma_start(ov[t], X[:, t, :]).then_inc(s_out, 16)
            sp.wait_ge(s_out, B * NT * 16)

        @block.gpsimd
        def _(pool):
            nc.gpsimd.memset(ident[:], 0.0).then_inc(s_const0, 1)
            nc.gpsimd.memset(causal16[:], 0.0).then_inc(s_const0, 1)
            nc.gpsimd.memset(mhalf[:], -0.5).then_inc(s_const, 1)
            nc.gpsimd.memset(wq_g[:], 0.0).then_inc(s_pad, 1)
            nc.gpsimd.memset(wk_g[:], 0.0).then_inc(s_pad, 1)
            nc.gpsimd.memset(bq_g[:], 0.0).then_inc(s_pad, 1)
            nc.gpsimd.memset(bk_g[:], 0.0).then_inc(s_pad, 1)
            nc.gpsimd.memset(ones4[:], 1.0).then_inc(s_pad, 1)
            nc.gpsimd.memset(VX[:, :, :, XE:XE + 1], 1.0).then_inc(s_vones, 1)
            nc.gpsimd.memset(MX[:], 0.0).then_inc(s_vones, 1)
            pool.wait_ge(s_const0, 2)
            nc.gpsimd.affine_select(out=ident[:], in_=ident[:], compare_op=ALU.not_equal, fill=1.0,
                                    base=0, pattern=[[-1, P]], channel_multiplier=1).then_inc(s_const, 1)
            nc.gpsimd.affine_select(out=causal16[:], in_=causal16[:], compare_op=ALU.is_ge, fill=NEG,
                                    base=0, pattern=[[-1, P]], channel_multiplier=1).then_inc(s_const, 1)
            nc.gpsimd.memset(ones16[:], 1.0).then_inc(s_const, 1)
            nc.gpsimd.memset(lower8[:], 1.0).then_inc(s_const0, 1)
            nc.gpsimd.memset(before16[:], 1.0).then_inc(s_const0, 1)
            nc.gpsimd.iota(region_i, pattern=[[REGION, E]], base=1, channel_multiplier=0).then_inc(s_const0, 1)
            nc.gpsimd.iota(tile_i[:], pattern=[[P, 2]], base=0, channel_multiplier=1).then_inc(s_const0, 1)
            pool.wait_ge(s_const, 3)
            nc.gpsimd.tensor_copy(ident16[:], ident[:]).then_inc(s_const, 1)
            pool.wait_ge(s_const0, 6)
            nc.gpsimd.affine_select(out=lower8[:], in_=lower8[:], compare_op=ALU.is_gt, fill=0.0,
                                    base=0, pattern=[[1, GR], [-1, GR]], channel_multiplier=0).then_inc(s_const, 1)
            nc.gpsimd.affine_select(out=before16[:], in_=before16[:], compare_op=ALU.is_gt, fill=0.0,
                                    base=0, pattern=[[1, P]], channel_multiplier=-1).then_inc(s_const, 1)
            nc.gpsimd.tensor_copy(region1[:], region_i).then_inc(s_const, 1)
            nc.gpsimd.tensor_copy(tile_no[:], tile_i[:]).then_inc(s_const0, 1)
            nc.gpsimd.memset(CNT[:], 0.0).then_inc(s_const0, 1)
            pool.dma_start(table[0:P, 0:2], tile_i[:]).then_inc(s_scat.sem, 16)
            with pool.Fori(0, B) as b:
                pool.wait_ge(s_var.sem, s_var.value(b, 1))
                nc.gpsimd.tensor_tensor(rstd[:, 0:NT], vep[:, 0:NT], mhalf[:, 0:NT], ALU.pow).then_inc(s_rstd.sem, 1)
                pool.wait_ge(s_cvar.sem, s_cvar.value(b, 1))
                nc.gpsimd.tensor_tensor(c_rstd[:], c_vep[:], mhalf[:], ALU.pow).then_inc(s_crstd.sem, 1)
                pool.wait_ge(s_crstd.sem, s_crstd.value(b, 1))
                nc.gpsimd.tensor_tensor(pool_scratch[:], mhalf[:, 0:1], mhalf[:, 0:1], ALU.mult)
                for i in range(SC):
                    last = nc.gpsimd.tensor_scalar(C[:, i, :], C[:, i, :], c_mv[:, i, 0:1], c_rstd[:, i:i + 1],
                                                   ALU.subtract, ALU.mult)
                last.then_inc(s_cn.sem, 1)

                def row_rstd(n):
                    pool.wait_ge(s_var.sem, s_var.value(b, n + 1))
                    nc.gpsimd.tensor_tensor(rstd[:, 0:NT], vep[:, 0:NT], mhalf[:, 0:NT], ALU.pow).then_inc(s_rstd.sem, 1)

                row_rstd(1)
                row_rstd(2)
                row_rstd(3)
                row_rstd(4)
                pool.wait_ge(s_ix.sem, s_ix.value(b, 1))
                nc.gpsimd.tensor_tensor(pool_scratch2[:], mhalf[:, 0:1], mhalf[:, 0:1], ALU.mult)
                for i in range(NT):
                    for j in range(K):
                        nc.gpsimd.indirect_dma_start(
                            out=rows_in, out_offset=bass.IndirectOffsetOnAxis(ap=IDXB[:, i, j:j + 1], axis=0),
                            in_=xr[:, i, :], in_offset=None).then_inc(s_scat.sem, 16)

            pool.wait_ge(s_tabl, 16)
            pool.wait_ge(s_zero, 16)

            def may_load(t):
                expert = pool.value_load(TROW[0:1, bass.ds(t * FIELDS + 3, 1)], min_val=0, max_val=E)
                pool.wait_ge(w_ready, expert)
                nc.gpsimd.sem_inc(e_may, 1)

            for t in range(LOADED):
                may_load(t)
            with pool.Fori(0, TILES // SLOTS) as n:
                for u in range(SLOTS):
                    t = n * SLOTS + u
                    may_load(t + LOADED)
                    if u % 2:
                        pool.wait_ge(e_O, t + 1 + 2)
                        pool.dma_start(rows_out[bass.ds((t - 1) * P, 2 * P), :].rearrange("(i p) d -> p i d", p=P),
                                       OS2[u // 2]).then_inc(e_st[u // 2], 16)

            for i in range(2):
                pool.wait_ge(e_st[i], 16 * (TILES // SLOTS))
            pool.wait_ge(e_T, TILES + 4)
            nc.gpsimd.sem_inc(g_use, K)
            pool.wait_ge(s_idx, 4 * B * NT * PARTS)
            with pool.Fori(0, B) as n:
                pool.wait_ge(g_use, n * (NT * K) + K)
                nc.gpsimd.tensor_copy(IDXB[:], IDX[:, bass.ds(n * NT, NT), 0:K]).then_inc(s_copied, 1)
                pool.wait_ge(s_copied, n + 1)
                for i in range(NT):
                    for j in range(K):
                        if j % HALF == 0:
                            at = 2 * i + j // HALF
                            pool.wait_ge(g_use, n * (NT * K) + i * K + j + HALF)
                            nc.gpsimd.tensor_tensor(carry[:, at:at + 1], mhalf[:, 0:1], mhalf[:, 0:1], ALU.mult)
                        nc.gpsimd.indirect_dma_start(
                            out=G[j], out_offset=None, in_=rows_out,
                            in_offset=bass.IndirectOffsetOnAxis(ap=IDXB[:, i, j:j + 1], axis=0)).then_inc(g_ld[j], 16)

        @block.scalar
        def _(act):
            act.wait_ge(ld_small, 48)
            context = a["ctx_1024"].rearrange("b (i p) d -> b p i d", p=P)
            with act.Fori(0, B) as b:
                act.wait_ge(s_batch, b + 1)
                act.dma_start(C[:], context[b]).then_inc(ld_ctx.sem, 16)
                act.wait_ge(s_kv.sem, s_kv.value(b, 1))
                nc.scalar.copy(V[:].rearrange("p i d -> p (i d)"), bank(1)).then_inc(s_kva.sem, 1)

                def probs_t(h):
                    act.wait_ge(s_t.sem, s_t.value(b, h + 1))
                    if h:
                        act.wait_ge(s_pv.sem, s_pv.value(b, h))
                    for j in (1, 2, 3):
                        n = T - P * j
                        last = nc.scalar.copy(PT[:, PT_AT[j]:PT_AT[j] + n], T_PS[j])
                    last.then_inc(s_pta.sem, 1)

                def attn_t(h):
                    act.wait_ge(s_pv.sem, s_pv.value(b, h + 1))
                    nc.scalar.activation(OT[:, h, :], bank(7), ACT.Identity, bias=bkv[:, 1:2]).then_inc(s_oe.sem, 1)

                for h in range(H):
                    if h:
                        probs_t(h - 1)
                    act.wait_ge(s_nb.sem, s_nb.value(b, h + 1))
                    if h >= 2:
                        act.wait_ge(s_t.sem, s_t.value(b, h - 1))
                    for i in range(NT):
                        n = P * (i + 1)
                        last = nc.scalar.activation(PR[h % 2][:, P_AT[i]:P_AT[i] + n], S_PS[i], ACT.Exp,
                                                    bias=nb[:, i:i + 1], scale=SELF_SCALE,
                                                    accum_out=rsum[:, i:i + 1])
                    last.then_inc(s_exp.sem, 1)
                    if h:
                        attn_t(h - 1)
                probs_t(H - 1)
                attn_t(H - 1)

                act.wait_ge(ld_cross, CROSS_LOADS * 16)
                act.wait_ge(s_cT.sem, s_cT.value(b, 1))
                for c in range(DC):
                    last = nc.scalar.activation(CT[:, c, :], PS[:, 2 * c * BANK:2 * (c + 1) * BANK], ACT.Identity,
                                                bias=norm_b[:, c:c + 1], scale=norm_w[:, c:c + 1])
                last.then_inc(s_cTe.sem, 1)

                def high_k(g, half):
                    act.wait_ge(s_pk[half].sem, s_pk[half].value(b, g + 1))
                    nc.scalar.activation(k_hi[:, half * T:(half + 1) * T], bank(half), ACT.Identity,
                                         bias=bk_g[:, g:g + 1]).then_inc(s_hi.sem, 1)

                def high_q(g):
                    act.wait_ge(s_pq.sem, s_pq.value(b, g + 1))
                    nc.scalar.activation(q_hi[:], bank(7), ACT.Identity, bias=bq_g[:, g:g + 1]).then_inc(s_hi.sem, 1)
                    if g:
                        act.wait_ge(s_qr.sem, s_qr.value(b, g))
                    nc.scalar.activation(q_whole[:], bank(7), ACT.Identity, bias=bq_g[:, g:g + 1]).then_inc(s_qw.sem, 1)

                def max_high(g):
                    st = s_stack[g % 2]
                    for j in range(HG):
                        act.wait_ge(st[j].sem, st[j].value(b, g // 2 + 1))
                    act.wait_ge(s_mT.sem, s_mT.value(b, g + 1))
                    if g:
                        act.wait_ge(s_aug.sem, s_aug.value(b, g))
                    nc.scalar.mul(m_hi[:], bank(7), -1.0).then_inc(s_mh.sem, 1)

                act.wait_ge(s_scat.sem, s_scat.value(b, 1))
                for g in range(2):
                    high_k(g, 0)
                    high_k(g, 1)
                    high_q(g)
                    if g == 0:
                        max_high(0)
                for g in range(NG):
                    for u in range(SC * 2):
                        n = g * SC * 2 + u
                        act.wait_ge(s_st.sem, s_st.value(b, n + 1))
                        if n >= 2:
                            act.wait_ge(s_pvx.sem, s_pvx.value(b, n - 1))
                        pair = PS[:, (2 + 2 * (u % 2)) * BANK:(4 + 2 * (u % 2)) * BANK]
                        nc.scalar.activation(PX[u % 2][:].rearrange("p j l -> p (j l)"), pair, ACT.Exp,
                                             scale=CROSS_SCALE).then_inc(s_ex.sem, 1)
                        if u == MAX_UNITS + 2 and g + 1 < NG:
                            max_high(g + 1)
                        if u in (MAX_UNITS + 3, MAX_UNITS + 4) and g + 2 < NG:
                            high_k(g + 2, u - MAX_UNITS - 3)
                        if u == MAX_UNITS + 5 and g + 2 < NG:
                            high_q(g + 2)

                act.wait_ge(s_lg.sem, s_lg.value(b, 1))
                nc.scalar.activation(SCR.rearrange("p i e -> p (i e)"), bank(0, 0, NT * E), ACT.Exp,
                                     scale=-1.0).then_inc(s_ez.sem, 1)
                act.wait_ge(s_gu.sem, s_gu.value(b, 1))
                nc.scalar.activation(s_gate, bank(2), ACT.Silu).then_inc(s_sg.sem, 1)

            act.wait_ge(s_tabl, 16)

            def load_tile(t, slot):
                row = act.value_load(TROW[0:1, bass.ds(t * FIELDS, 1)], min_val=0, max_val=E * REGION)
                act.wait_ge(e_may, t + 1)
                act.dma_start(XS[slot], rows_in[bass.ds(row, P), :]).then_inc(e_ld[slot], 16)

            def silu(t, u):
                act.wait_ge(e_GU, t + 1)
                nc.scalar.activation(SG[u % 2], bank(2 + u % 2, 0, F), ACT.Silu).then_inc(e_SG, 1)

            def hidden_t(t, u):
                act.wait_ge(e_HP, t + 1)
                nc.scalar.copy(HT[u % 2], bank(4 + u % 2, 0, P)).then_inc(e_HT, 1)

            def act_tiles(n, last=False):
                for u in range(LOADED):
                    t = n * LOADED + u
                    silu(t + 2, u)
                    hidden_t(t + 1, u + 1)
                    if not last or u < 4:
                        load_tile(t + LOADED, u)

            for t in range(LOADED):
                load_tile(t, t)
            silu(0, 0)
            silu(1, 1)
            hidden_t(0, 0)
            with act.Fori(0, TILES // LOADED - 1) as n:
                act_tiles(n)
            act_tiles(TILES // LOADED - 1, last=True)

        @block.vector
        def _(dve):
            nc.vector.memset(PX[0][:], 0.0).then_inc(s_qm0, 1)
            dve.wait_ge(s_qm0, 1)
            for j in range(HG):
                nc.vector.tensor_copy(QM[:, j, :], PX[0][:, 0, :]).then_inc(s_qm0, 1)
            dve.wait_ge(s_qm0, 1 + HG)
            dve.wait_ge(s_const, N_CONST)
            dve.wait_ge(ld_small, 48)
            dve.wait_ge(s_vones, 2)
            dve.wait_ge(s_const0, 8)
            nc.vector.sem_inc(s_batch, 1)
            dve.wait_ge(ld_x[0], 16)
            with dve.Fori(0, B) as b:
                n_links = [0]

                def link(ins):
                    n_links[0] += 1
                    ins.then_inc(s_dve.sem, 1)

                def linked():
                    dve.wait_ge(s_dve.sem, s_dve.value(b, n_links[0]))

                def settle():
                    linked()
                    link(nc.vector.memset(scratch[:], 0.0))

                norms = [0]

                def row_norm(src, dst, tiles=NT):
                    norms[0] += 1
                    for i in range(tiles):
                        link(nc.vector.bn_stats(stats[:, i, :], src(i)))
                    settle()
                    for i in range(tiles):
                        link(nc.vector.bn_aggr(mv[:, i, :], stats[:, i, :]))
                    linked()
                    nc.vector.tensor_scalar(vep[:, 0:tiles], mv[:, 0:tiles, 1], EPS, None, ALU.add).then_inc(s_var.sem, 1)
                    dve.wait_ge(s_rstd.sem, s_rstd.value(b, norms[0]))
                    for i in range(tiles):
                        last = nc.vector.tensor_scalar(dst(i), src(i), mv[:, i, 0:1], rstd[:, i:i + 1],
                                                       ALU.subtract, ALU.mult)
                    return last

                def x_row(i):
                    return X[:, b * NT + i, :]

                def xn_row(i):
                    return xn[:, i, :]

                row_norm(x_row, xn_row).then_inc(s_xn.sem, 1)
                dve.wait_ge(s_xnT.sem, s_xnT.value(b, 1))
                nc.vector.tensor_copy(xnT[:].rearrange("p c t -> p (c t)"), PS[:, 5 * BANK:7 * BANK]).then_inc(s_xnTe.sem, 1)
                dve.wait_ge(s_kv.sem, s_kv.value(b, 1))
                nc.vector.scalar_tensor_tensor(KT[:], bank(7), bkv[:, 0:1], peT[:], ALU.add, ALU.add).then_inc(s_kvd.sem, 1)

                def q_t(h):
                    dve.wait_ge(s_q.sem, s_q.value(b, h + 1))
                    if h >= 2:
                        dve.wait_ge(s_s.sem, s_s.value(b, h - 1))
                    nc.vector.scalar_tensor_tensor(QT[h % 2][:], bank(0), bq[:, h:h + 1], peT[:],
                                                   ALU.add, ALU.add).then_inc(s_qe.sem, 1)

                def probs_t(h):
                    dve.wait_ge(s_t.sem, s_t.value(b, h + 1))
                    if h:
                        dve.wait_ge(s_pv.sem, s_pv.value(b, h))
                    nc.vector.tensor_copy(PT[:, 0:T], T_PS[0]).then_inc(s_ptd.sem, 1)

                q_t(0)
                dve.wait_ge(ld_ctx.sem, ld_ctx.value(b, 1))
                for i in range(SC):
                    link(nc.vector.bn_stats(c_stats[:, i, :], C[:, i, :]))
                settle()
                for i in range(SC):
                    link(nc.vector.bn_aggr(c_mv[:, i, :], c_stats[:, i, :]))
                linked()
                nc.vector.tensor_scalar(c_vep[:], c_mv[:, :, 1], EPS, None, ALU.add).then_inc(s_cvar.sem, 1)
                for h in range(H):
                    dve.wait_ge(s_s.sem, s_s.value(b, h + 1))
                    for i in range(NT):
                        link(nc.vector.tensor_reduce(mx[:, i:i + 1], S_PS[i], AX.X, ALU.max))
                    linked()
                    nc.vector.tensor_scalar(nb[:], mx[:], -SELF_SCALE, None, ALU.mult).then_inc(s_nb.sem, 1)
                    if h:
                        probs_t(h - 1)
                    if h + 1 < H:
                        q_t(h + 1)
                    dve.wait_ge(s_exp.sem, s_exp.value(b, h + 1))
                    link(nc.vector.reciprocal(rinv[:], rsum[:]))
                    linked()
                    for i in range(NT):
                        rows = PR[h % 2][:, P_AT[i]:P_AT[i] + P * (i + 1)]
                        last = nc.vector.tensor_scalar(rows, rows, rinv[:, i:i + 1], None, ALU.mult)
                    last.then_inc(s_norm.sem, 1)
                probs_t(H - 1)
                dve.wait_ge(s_wo.sem, s_wo.value(b, 1))
                for i in range(NT):
                    last = nc.vector.tensor_tensor(X[:, b * NT + i, :], X[:, b * NT + i, :],
                                                   bank(2 + i // 2, (i % 2) * D, (i % 2) * D + D), ALU.add)
                    link(last)
                settle()

                for i in range(1, B):
                    dve.wait_ge(ld_x[i], 16)
                dve.wait_ge(ld_cross, CROSS_LOADS * 16)
                dve.wait_ge(ld_ffn, FFN_LOADS * 16)

                link(row_norm(x_row, xn_row))
                linked()
                row_norm(xn_row, xn_row).then_inc(s_xn.sem, 1)

                def affine(first, w, bias):
                    for c in range(DC):
                        last = nc.vector.tensor_scalar(xnT[:, c, :], bank(first + c), w[:, c:c + 1], bias[:, c:c + 1],
                                                       ALU.mult, ALU.add)
                    last.then_inc(s_xnTe.sem, 1)

                dve.wait_ge(s_xnT.sem, s_xnT.value(b, 2))
                affine(4, norm_w, norm_b)
                dve.wait_ge(s_vx.sem, s_vx.value(b, 1))
                for n in range(4):
                    for i in range(2):
                        last = nc.vector.tensor_tensor(VX[:, 2 * n + i, :, 0:XE],
                                                       bank(n, i * D, i * D + D).rearrange("p (h e) -> p h e", e=XE),
                                                       bv_row[:].rearrange("p (h e) -> p h e", e=XE), ALU.add)
                last.then_inc(s_vxe.sem, 1)
                def low_parts(g):
                    for half in range(2):
                        dve.wait_ge(s_hi.sem, s_hi.value(b, 3 * g + half + 1))
                        cols = slice(half * T, (half + 1) * T)
                        nc.vector.scalar_tensor_tensor(k_lo[:, cols], bank(half), bk_g[:, g:g + 1],
                                                       k_hi[:, cols].bitcast(F32), ALU.add, ALU.subtract).then_inc(s_lo.sem, 1)
                    dve.wait_ge(s_hi.sem, s_hi.value(b, 3 * g + 3))
                    for j in range(HG):
                        head = slice(W * j, W * j + W)
                        last = nc.vector.tensor_copy(QM[head, j, :], q_hi[head, :])
                    last.then_inc(s_qm.sem, 1)
                    dve.wait_ge(s_qw.sem, s_qw.value(b, g + 1))
                    nc.vector.tensor_tensor(q_lo[:], q_whole[:], q_hi[:].bitcast(F32), ALU.subtract).then_inc(s_lo.sem, 1)

                def q_rows(g):
                    dve.wait_ge(s_qw.sem, s_qw.value(b, g + 1))
                    if g >= 2:
                        dve.wait_ge(s_o.sem, s_o.value(b, g - 1))
                    nc.vector.transpose(QR[g % 2][:], q_whole[:].rearrange("p (q m) -> p m q", m=XE)).then_inc(s_qr.sem, 1)

                def maxima(g, n):
                    half, i, j = n // (NT * HG), n // HG % NT, n % HG
                    k = g * 2 * NT * HG + n
                    dve.wait_ge(s_p1.sem, s_p1.value(b, k + 1))
                    nc.vector.tensor_reduce(MP[:, half, i, j:j + 1], bank(max_bank(g, n)), AX.X, ALU.max).then_inc(s_p1d.sem, 1)

                def max_columns(g):
                    dve.wait_ge(s_p1d.sem, s_p1d.value(b, (g + 1) * 2 * NT * HG))
                    if g:
                        dve.wait_ge(s_mT.sem, s_mT.value(b, g))
                    nc.vector.tensor_tensor(MX[:, :, :, XE], MP[:, 0], MP[:, 1], ALU.max).then_inc(s_mx.sem, 1)

                def max_low(g):
                    dve.wait_ge(s_mh.sem, s_mh.value(b, g + 1))
                    nc.vector.scalar_tensor_tensor(m_lo[:], bank(7), -1.0, m_hi[:].bitcast(F32),
                                                   ALU.mult, ALU.subtract).then_inc(s_ml.sem, 1)

                def out_rows(g):
                    dve.wait_ge(s_pvx.sem, s_pvx.value(b, (g + 1) * SC * 2))
                    nc.vector.transpose(OR[:], bank(6).rearrange("p (q m) -> p m q", m=XE)).then_inc(s_or.sem, 1)
                    dve.wait_ge(s_or.sem, s_or.value(b, g + 1))
                    link(nc.vector.reciprocal(RG[:], OR[:, :, XE]))
                    linked()
                    mine = O[:, g, :].rearrange("p (m e) -> p m e", e=XE)
                    link(nc.vector.tensor_tensor(mine, OR[:, :, 0:XE],
                                                 RG[:].unsqueeze(2).to_broadcast([P, XE, XE]), ALU.mult))
                    linked()
                    nc.vector.tensor_tensor(mine, mine, QR[g % 2][:, :, 0:XE], ALU.add).then_inc(s_o.sem, 1)

                low_parts(0)
                q_rows(0)
                for g in range(-1, NG):
                    if g >= 1:
                        out_rows(g - 1)
                    if 0 <= g < NG - 1:
                        q_rows(g + 1)
                    if g + 1 < NG:
                        for n in range(2 * NT * HG):
                            maxima(g + 1, n)
                        max_columns(g + 1)
                        max_low(g + 1)
                    if g + 2 < NG:
                        low_parts(g + 2)
                out_rows(NG - 1)
                dve.wait_ge(s_o.sem, s_o.value(b, NG))
                row_norm(lambda i: O[:, i, :], xn_row).then_inc(s_xn.sem, 1)
                for i in range(NT):
                    link(nc.vector.tensor_tensor(O[:, i, :], O[:, i, :], bo_row[:], ALU.add))
                dve.wait_ge(s_xnT.sem, s_xnT.value(b, 3))
                affine(4, norm1_w, norm1_b)
                linked()
                for i in range(NT):
                    link(nc.vector.tensor_tensor(x_row(i), x_row(i), O[:, i, :], ALU.add))
                linked()
                dve.wait_ge(s_xo.sem, s_xo.value(b, 1))
                for i in range(NT):
                    link(nc.vector.tensor_tensor(x_row(i), x_row(i),
                                                 bank(2 + i // 2, (i % 2) * D, (i % 2) * D + D), ALU.add))

                dve.wait_ge(s_scat.sem, s_scat.value(b, 1))
                settle()
                row_norm(x_row, lambda i: xr[:, i, :]).then_inc(s_xn.sem, 1)
                dve.wait_ge(s_xnT.sem, s_xnT.value(b, 4))
                nc.vector.tensor_copy(xnT[:].rearrange("p c t -> p (c t)"), PS[:, 4 * BANK:6 * BANK]).then_inc(s_xnTe.sem, 1)

                def each(ap):
                    return ap.rearrange("p i e -> p (i e)")

                def over_tiles(row):
                    return row.unsqueeze(1).to_broadcast([P, NT, E])

                dve.wait_ge(s_ez.sem, s_ez.value(b, 1))
                link(nc.vector.tensor_scalar(each(SWB), each(SCR), 1.0, None, ALU.add))
                linked()
                link(nc.vector.reciprocal(each(SCR), each(SWB)))
                linked()
                link(nc.vector.tensor_tensor(SWB, SCR, over_tiles(br_row[:]), ALU.add))
                settle()
                for i in range(NT):
                    for g in range(E // GR):
                        link(nc.vector.max(SRT[:, i, g, :], SWB[:, i, g * GR:(g + 1) * GR]))
                linked()
                link(nc.vector.tensor_tensor(GS[:], SRT[:, :, :, 0], SRT[:, :, :, 1], ALU.add))
                linked()
                other = GS[:].unsqueeze(2).to_broadcast([P, NT, GR, GR])
                own = GS[:].unsqueeze(3).to_broadcast([P, NT, GR, GR])
                link(nc.vector.tensor_tensor(CMP, other, own, ALU.is_gt))
                link(nc.vector.tensor_tensor(CMQ, other, own, ALU.is_equal))
                linked()
                link(nc.vector.tensor_tensor(CMQ, CMQ, lower8[:].unsqueeze(1).to_broadcast([P, NT, GR, GR]), ALU.mult))
                linked()
                link(nc.vector.tensor_tensor(CMP, CMP, CMQ, ALU.add))
                linked()
                link(nc.vector.tensor_reduce(GS[:], CMP, AX.X, ALU.add))
                linked()
                link(nc.vector.tensor_scalar(GS[:], GS[:], 3.5, None, ALU.is_lt))
                linked()
                grouped = SWB.rearrange("p i (g e) -> p i g e", e=GR)
                link(nc.vector.tensor_tensor(grouped, grouped, GS[:].unsqueeze(3).to_broadcast([P, NT, GR, GR]), ALU.mult))
                settle()
                for i in range(NT):
                    link(nc.vector.max(TOP[:, i, :], SWB[:, i, :]))
                settle()
                for i in range(NT):
                    link(nc.vector.match_replace(SEL[:, i, :], TOP[:, i, :], SWB[:, i, :], NEG))
                linked()
                link(nc.vector.tensor_scalar(each(SEL), each(SEL), NEG / 10, None, ALU.is_lt))
                linked()
                nc.vector.tensor_copy(each(SEL16[:]), each(SEL)).then_inc(s_sel.sem, 1)
                dve.wait_ge(s_sg.sem, s_sg.value(b, 1))
                nc.vector.tensor_tensor(s_hid, s_gate, bank(3), ALU.mult).then_inc(s_sh.sem, 1)
                link(nc.vector.tensor_tensor(SCR, SCR, SEL, ALU.mult))
                linked()
                link(nc.vector.tensor_reduce(WSUM[:], SCR, AX.X, ALU.add))
                linked()
                link(nc.vector.tensor_scalar(WSUM[:], WSUM[:], 1e-20, None, ALU.add))
                linked()
                link(nc.vector.reciprocal(WSUM[:], WSUM[:]))
                linked()
                link(nc.vector.tensor_scalar(WSUM[:], WSUM[:], ROUTED, None, ALU.mult))
                linked()
                link(nc.vector.tensor_tensor(SCR, SCR, WSUM[:].unsqueeze(2).to_broadcast([P, NT, E]), ALU.mult))
                link(nc.vector.tensor_tensor(BASE, CNT[:], region1[:], ALU.add))
                linked()
                dve.wait_ge(s_rk.sem, s_rk.value(b, 1))
                link(nc.vector.tensor_tensor(SWB, bank(1, 0, NT * E).rearrange("p (i e) -> p i e", i=NT),
                                             over_tiles(BASE), ALU.add))
                link(nc.vector.tensor_tensor(CNT[:], CNT[:], bank(1, NT * E, (NT + 1) * E), ALU.add))
                linked()
                link(nc.vector.tensor_tensor(SWB, SWB, SEL, ALU.mult))
                settle()
                for i in range(NT):
                    link(nc.vector.max(V8[:, i, :], SWB[:, i, :]))
                linked()
                link(nc.vector.tensor_copy(SLOT1[:, bass.ds(b * NT, NT), 0:K], V8[:]))
                nc.vector.tensor_scalar(IDXB[:], V8[:], -1.0, None, ALU.add).then_inc(s_ix.sem, 1)
                for i in range(NT):
                    linked()
                    link(nc.vector.tensor_tensor(EQ, SWB[:, i, :].unsqueeze(1).to_broadcast([P, K, E]),
                                                 V8[:, i, :].unsqueeze(2).to_broadcast([P, K, E]), ALU.is_equal))
                    linked()
                    link(nc.vector.tensor_tensor(EQ, EQ, SCR[:, i, :].unsqueeze(1).to_broadcast([P, K, E]), ALU.mult))
                    linked()
                    link(nc.vector.tensor_reduce(WTS[:, b * NT + i, :], EQ, AX.X, ALU.add))
                dve.wait_ge(s_sd.sem, s_sd.value(b, 1))
                for i in range(NT):
                    link(nc.vector.tensor_tensor(x_row(i), x_row(i),
                                                 bank(6 + i // 2, (i % 2) * D, (i % 2) * D + D), ALU.add))
                linked()
                nc.vector.sem_inc(s_dve.sem, s_dve.per_batch - n_links[0])
                nc.vector.sem_inc(s_batch, 1)

            steps = [0]

            def then(ins):
                ins.then_inc(s_tabc, 1)
                steps[0] += 1
                dve.wait_ge(s_tabc, steps[0])

            then(nc.vector.tensor_scalar(TI, CNT[:], float(P - 1), None, ALU.add))
            then(nc.vector.tensor_scalar(TI, TI, 7, None, ALU.logical_shift_right))
            then(nc.vector.tensor_copy(TF, TI))
            then(nc.vector.memset(ZERO, 0.0))
            then(nc.vector.memset(SLOT1[:, :, K:PARTS * PK], 1.0))
            then(nc.vector.memset(IND[:, 0, :], 1.0))
            then(nc.vector.tensor_tensor_scan(CUM, IND[:, 0, :], TF, 0.0, ALU.mult, ALU.add))
            then(nc.vector.tensor_scalar(NEED, CUM, 1.0, None, ALU.add))
            then(nc.vector.tensor_copy(COUNT_I, CNT[:]))
            for h in range(2):
                then(nc.vector.tensor_scalar(IND[:, h, :], CUM, tile_no[:, h:h + 1], None, ALU.is_le))
                then(nc.vector.tensor_reduce(TE[:, h:h + 1], IND[:, h, :], AX.X, ALU.add))
                then(nc.vector.tensor_tensor(IND[:, h, :], IND[:, h, :], TF, ALU.mult))
                then(nc.vector.tensor_reduce(TX[:, h:h + 1], IND[:, h, :], AX.X, ALU.add))
            then(nc.vector.tensor_tensor(TX[:], tile_no[:], TX[:], ALU.subtract))
            then(nc.vector.tensor_scalar(TX[:], TX[:], float(P), None, ALU.mult))
            then(nc.vector.scalar_tensor_tensor(TBF[:, :, 1], TE[:], float(REGION), TX[:], ALU.mult, ALU.add))
            then(nc.vector.tensor_scalar(TBF[:, :, 0], TBF[:, :, 1], float(E * REGION), None, ALU.min))
            then(nc.vector.tensor_scalar(TBF[:, :, 2], TE[:], float(E - 1), None, ALU.min))
            then(nc.vector.tensor_scalar(TBF[:, :, 3], TBF[:, :, 2], 1.0, None, ALU.add))
            then(nc.vector.memset(DD[:, 0:1], 0.0))
            then(nc.vector.tensor_scalar(DD[:, 1:E], TF[:, 0:E - 1], float(P), float(-REGION), ALU.mult, ALU.add))
            then(nc.vector.tensor_copy(TB[:], TBF[:]))
            then(nc.vector.tensor_scalar(TB[:, :, 2], TB[:, :, 2], RING - 1, None, ALU.bitwise_and))
            nc.vector.sem_inc(s_tab, 1)

            def tile_t(t, u):
                dve.wait_ge(e_T, t + 1)
                nc.vector.tensor_copy(XT[u % SLOTS], bank(u % 2, 0, D)).then_inc(e_XT, 1)

            def hidden(t, u):
                dve.wait_ge(e_SG, t + 1)
                nc.vector.tensor_tensor(HH[u % 2], SG[u % 2], bank(2 + u % 2, F, 2 * F), ALU.mult).then_inc(e_H, 1)

            nc.vector.sem_inc(e_O, 2)
            for t in range(4):
                tile_t(t, t)
            for t in range(2):
                hidden(t, t)

            def dve_tile(turn, u, first):
                t = turn * SLOTS + u
                tile_t(t + 4, u)
                hidden(t + 2, u)
                dve.wait_ge(e_D, t + 2)
                if u % 2 == 0 and not first:
                    dve.wait_ge(e_st[u // 2], turn * 16)
                nc.vector.tensor_copy(OS[u], bank(6 + u % 2, 0, D)).then_inc(e_O, 1)

            def tiles_and_rows(m, part, first=False):
                cols = slice(part * PK, part * PK + PK)
                turn, step = m + part * B * NT, m * 4 + part * B * NT * 4
                dve_tile(turn, 0, first)
                nc.vector.tensor_tensor(MOVE, SLOT1[:, m, cols].unsqueeze(2).to_broadcast([P, PK, E]),
                                        region1[:].unsqueeze(1).to_broadcast([P, PK, E]), ALU.is_ge).then_inc(s_idx, 1)
                dve_tile(turn, 1, first)
                dve.wait_ge(s_idx, step + 1)
                nc.vector.tensor_tensor(MOVE, MOVE, DD.unsqueeze(1).to_broadcast([P, PK, E]), ALU.mult).then_inc(s_idx, 1)
                dve_tile(turn, 2, first)
                dve.wait_ge(s_idx, step + 2)
                nc.vector.tensor_reduce(V8[:, 0, 0:PK], MOVE, AX.X, ALU.add).then_inc(s_idx, 1)
                dve_tile(turn, 3, first)
                dve.wait_ge(s_idx, step + 3)
                nc.vector.scalar_tensor_tensor(IDX[:, m, cols], SLOT1[:, m, cols], -1.0, V8[:, 0, 0:PK],
                                               ALU.add, ALU.add).then_inc(s_idx, 1)
                dve.wait_ge(s_idx, step + 4)

            tiles_and_rows(0, 0, first=True)
            for part in range(PARTS):
                with dve.Fori(1 if part == 0 else 0, B * NT) as m:
                    tiles_and_rows(m, part)

            with dve.Fori(0, B * NT) as t:
                for j in range(K):
                    dve.wait_ge(g_ld[j], t * 16 + 16)
                    dve.wait_ge(g_use, t * K + K + j)
                    last = nc.vector.scalar_tensor_tensor(X[:, t, :], G[j], WTS[:, t, j:j + 1], X[:, t, :],
                                                          ALU.mult, ALU.add).then_inc(g_use, 1)
                dve.wait_ge(g_use, t * K + 2 * K)
                nc.vector.sem_inc(s_fin, 1)

        @block.tensor
        def _(pe):
            pe.wait_ge(s_const, N_CONST)
            pe.wait_ge(ld_wqkv, 32)
            pe.wait_ge(ld_wo, 16)
            with pe.Fori(0, B) as b:
                pe.wait_ge(s_batch, b + 1)

                def transpose_rows(src, tiles, first_bank):
                    for c in range(DC):
                        for i in range(tiles):
                            at = (first_bank + c * (tiles // NT)) * BANK + i * P
                            last = nc.tensor.transpose(PS[:, at:at + P], src[:, i, c * P:(c + 1) * P], ident[:])
                    return last

                pe.wait_ge(s_xn.sem, s_xn.value(b, 1))
                transpose_rows(xn, NT, 5).then_inc(s_xnT.sem, 1)
                pe.wait_ge(s_xnTe.sem, s_xnTe.value(b, 1))
                for c in range(DC):
                    nc.tensor.matmul(bank(7), wkv[:, c, 0:HD], xnT[:, c, :], start=(c == 0), stop=(c == DC - 1))
                for i in range(NT):
                    for c in range(DC):
                        last = nc.tensor.matmul(bank(1, i * P, i * P + P), xnT[:, c, i * P:(i + 1) * P],
                                                wkv[:, c, HD:2 * HD], start=(c == 0), stop=(c == DC - 1))
                last.then_inc(s_kv.sem, 1)

                def q_proj(h):
                    if h:
                        pe.wait_ge(s_qe.sem, s_qe.value(b, h))
                    for c in range(DC):
                        last = nc.tensor.matmul(bank(0), wq[:, c, h * HD:(h + 1) * HD], xnT[:, c, :],
                                                start=(c == 0), stop=(c == DC - 1))
                    last.then_inc(s_q.sem, 1)

                def scores(h):
                    pe.wait_ge(s_qe.sem, s_qe.value(b, h + 1))
                    if h == 0:
                        pe.wait_ge(s_kvd.sem, s_kvd.value(b, 1))
                    else:
                        pe.wait_ge(s_exp.sem, s_exp.value(b, h))
                    for i in range(NT):
                        nc.tensor.matmul(S_PS[i], QT[h % 2][:, i * P:(i + 1) * P], KT[:, 0:P * (i + 1)],
                                         start=True, stop=False)
                        last = nc.tensor.matmul(S_PS[i][:, P * i:P * (i + 1)], ident16[:], causal16[:],
                                                start=False, stop=True)
                    last.then_inc(s_s.sem, 1)

                def transposes(h):
                    pe.wait_ge(s_norm.sem, s_norm.value(b, h + 1))
                    if h:
                        pe.wait_ge(s_ptd.sem, s_ptd.value(b, h))
                        pe.wait_ge(s_pta.sem, s_pta.value(b, h))
                    else:
                        pe.wait_ge(s_kva.sem, s_kva.value(b, 1))
                    for j in range(NT):
                        for i in range(j, NT):
                            last = nc.tensor.transpose(T_PS[j][:, P * (i - j):P * (i - j + 1)],
                                                       PR[h % 2][:, P_AT[i] + P * j:P_AT[i] + P * (j + 1)], ident[:])
                    last.then_inc(s_t.sem, 1)

                def attn(h):
                    pe.wait_ge(s_ptd.sem, s_ptd.value(b, h + 1))
                    pe.wait_ge(s_pta.sem, s_pta.value(b, h + 1))
                    if h:
                        pe.wait_ge(s_oe.sem, s_oe.value(b, h))
                    for j in range(NT):
                        last = nc.tensor.matmul(bank(7, P * j), V[:, j, :], PT[:, PT_AT[j]:PT_AT[j] + T - P * j],
                                                start=(j == 0), stop=(j == NT - 1))
                    last.then_inc(s_pv.sem, 1)

                q_proj(0)
                for h in range(H):
                    scores(h)
                    if h:
                        transposes(h - 1)
                    if h + 1 < H:
                        q_proj(h + 1)
                    if h:
                        attn(h - 1)
                transposes(H - 1)
                attn(H - 1)
                pe.wait_ge(s_oe.sem, s_oe.value(b, H))
                for i in range(NT):
                    for h in range(H):
                        last = nc.tensor.matmul(bank(2 + i // 2, (i % 2) * D, (i % 2) * D + D),
                                                OT[:, h, i * P:(i + 1) * P], wo[:, h, :],
                                                start=(h == 0), stop=(h == H - 1))
                last.then_inc(s_wo.sem, 1)

                pe.wait_ge(ld_cross, CROSS_LOADS * 16)
                pe.wait_ge(s_cn.sem, s_cn.value(b, 1))
                pe.wait_ge(s_xn.sem, s_xn.value(b, 2))
                transpose_rows(C, SC, 0).then_inc(s_cT.sem, 1)
                transpose_rows(xn, NT, 4).then_inc(s_xnT.sem, 1)
                pe.wait_ge(s_cTe.sem, s_cTe.value(b, 1))
                for n in range(SC):
                    for c in range(DC):
                        last = nc.tensor.matmul(bank(n // 2, (n % 2) * D, (n % 2) * D + D), CT[:, c, n * P:(n + 1) * P],
                                                xwv[:, c, :], start=(c == 0), stop=(c == DC - 1))
                last.then_inc(s_vx.sem, 1)
                pe.wait_ge(s_xnTe.sem, s_xnTe.value(b, 2))
                def project_k(g, half):
                    for c in range(DC):
                        last = nc.tensor.matmul(bank(half), wk_g[:, c, g, :], CT[:, c, half * T:(half + 1) * T],
                                                start=(c == 0), stop=(c == DC - 1))
                    last.then_inc(s_pk[half].sem, 1)

                def project_q(g):
                    if g:
                        pe.wait_ge(s_ml.sem, s_ml.value(b, g))
                    for c in range(DC):
                        last = nc.tensor.matmul(bank(7), wq_g[:, c, g, :], xnT[:, c, :],
                                                start=(c == 0), stop=(c == DC - 1))
                    last.then_inc(s_pq.sem, 1)

                def max_scores(g, n):
                    half, i, j = n // (NT * HG), n // HG % NT, n % HG
                    k = g * 2 * NT * HG + n
                    if n == 0:
                        pe.wait_ge(s_qm.sem, s_qm.value(b, g + 1))
                        pe.wait_ge(s_lo.sem, s_lo.value(b, 3 * g + 2))
                    if n == 2:
                        pe.wait_ge(s_qw.sem, s_qw.value(b, g + 1))
                    if n >= max_banks(g):
                        pe.wait_ge(s_p1d.sem, s_p1d.value(b, k + 1 - max_banks(g)))
                    nc.tensor.matmul(bank(max_bank(g, n)), QM[:, j, i * P:(i + 1) * P], k_hi[:, half * T:(half + 1) * T],
                                     start=True, stop=True).then_inc(s_p1.sem, 1)

                def max_rows(g):
                    pe.wait_ge(s_mx.sem, s_mx.value(b, g + 1))
                    pe.wait_ge(s_qw.sem, s_qw.value(b, g + 1))
                    for i in range(NT):
                        last = nc.tensor.transpose(bank(7, i * P, i * P + P), MX[:, i].rearrange("p j w -> p (j w)"), ident[:])
                    last.then_inc(s_mT.sem, 1)

                def cross_scores(g, u):
                    c, n = u // 2, g * 2 * SC + u
                    if u < 2:
                        pe.wait_ge(s_aug.sem, s_aug.value(b, g + 1))
                    if n >= 2:
                        pe.wait_ge(s_ex.sem, s_ex.value(b, n - 1))
                    for jj in range(2):
                        j = 2 * (u % 2) + jj
                        last = nc.tensor.matmul(bank(2 + 2 * (u % 2) + jj), KS[g % 2][:, j, c * P:(c + 1) * P],
                                                QS[g % 2][:, j, :], start=True, stop=True)
                    last.then_inc(s_st.sem, 1)

                def cross_pv(g, u):
                    c, n = u // 2, g * 2 * SC + u
                    pe.wait_ge(s_ex.sem, s_ex.value(b, n + 1))
                    if u < 2 and g:
                        pe.wait_ge(s_or.sem, s_or.value(b, g))
                    for jj in range(2):
                        j = 2 * (u % 2) + jj
                        last = nc.tensor.matmul(PS[W * j:W * j + XE + 1, 6 * BANK:7 * BANK], VX[:, c, HG * g + j, :],
                                                PX[u % 2][:, jj, :], start=(c == 0), stop=(c == SC - 1))
                    last.then_inc(s_pvx.sem, 1)

                pe.wait_ge(s_vxe.sem, s_vxe.value(b, 1))
                project_k(0, 0)
                project_k(0, 1)
                project_q(0)
                for n in range(2 * NT * HG):
                    max_scores(0, n)
                max_rows(0)
                project_k(1, 0)
                project_k(1, 1)
                project_q(1)
                for g in range(NG):
                    cross_scores(g, 0)
                    cross_scores(g, 1)
                    for u in range(2 * SC):
                        now = []
                        if u < MAX_UNITS and g + 1 < NG:
                            now = list(range(2 * NT * HG * u // MAX_UNITS, 2 * NT * HG * (u + 1) // MAX_UNITS))
                        for n in now[:1]:
                            max_scores(g + 1, n)
                        cross_pv(g, u)
                        for n in now[1:2]:
                            max_scores(g + 1, n)
                        if u + 2 < 2 * SC:
                            cross_scores(g, u + 2)
                        for n in now[2:]:
                            max_scores(g + 1, n)
                        if u == MAX_UNITS and g + 1 < NG:
                            max_rows(g + 1)
                        if u in (MAX_UNITS + 1, MAX_UNITS + 2) and g + 2 < NG:
                            project_k(g + 2, u - MAX_UNITS - 1)
                        if u == MAX_UNITS + 3 and g + 2 < NG:
                            project_q(g + 2)
                pe.wait_ge(s_xn.sem, s_xn.value(b, 3))
                transpose_rows(xn, NT, 4).then_inc(s_xnT.sem, 1)
                pe.wait_ge(s_xnTe.sem, s_xnTe.value(b, 3))
                for i in range(NT):
                    for c in range(DC):
                        last = nc.tensor.matmul(bank(2 + i // 2, (i % 2) * D, (i % 2) * D + D),
                                                xnT[:, c, i * P:(i + 1) * P], xwo[:, c, :],
                                                start=(c == 0), stop=(c == DC - 1))
                last.then_inc(s_xo.sem, 1)

                pe.wait_ge(s_xn.sem, s_xn.value(b, 4))
                transpose_rows(xr, NT, 4).then_inc(s_xnT.sem, 1)
                pe.wait_ge(s_xnTe.sem, s_xnTe.value(b, 4))
                for i in range(NT):
                    for c in range(DC):
                        last = nc.tensor.matmul(bank(0, i * E, (i + 1) * E), xnT[:, c, i * P:(i + 1) * P], wr[:, c, :],
                                                start=(c == 0), stop=(c == DC - 1))
                last.then_inc(s_lg.sem, 1)
                for n in range(2):
                    for c in range(DC):
                        last = nc.tensor.matmul(bank(2 + n), ws_gu[:, c, n * F:(n + 1) * F], xnT[:, c, :],
                                                start=(c == 0), stop=(c == DC - 1))
                last.then_inc(s_gu.sem, 1)
                pe.wait_ge(s_sel.sem, s_sel.value(b, 1))
                for i in range(NT):
                    for k in range(i + 1):
                        nc.tensor.matmul(bank(1, i * E, (i + 1) * E), before16[:] if k == i else ones16[:],
                                         SEL16[:, k, :], start=(k == 0), stop=(k == i))
                for k in range(NT):
                    last = nc.tensor.matmul(bank(1, NT * E, (NT + 1) * E), ones16[:], SEL16[:, k, :],
                                            start=(k == 0), stop=(k == NT - 1))
                last.then_inc(s_rk.sem, 1)
                pe.wait_ge(s_sh.sem, s_sh.value(b, 1))
                for i in range(NT):
                    last = nc.tensor.matmul(bank(6 + i // 2, (i % 2) * D, (i % 2) * D + D),
                                            s_hid[:, i * P:(i + 1) * P], ws_d[:], start=True, stop=True)
                last.then_inc(s_sd.sem, 1)

            pe.wait_ge(s_batch, B + 1)
            pe.wait_ge(s_tabl, 16)
            nc.tensor.sem_inc(e_D, 1)

            def transposes_of(slot, bank_no, loaded):
                pe.wait_ge(e_ld[slot], loaded)
                for c in range(DC):
                    last = nc.tensor.transpose(bank(bank_no, c * P, (c + 1) * P), XS[slot][:, c * P:(c + 1) * P], ident[:])
                last.then_inc(e_T, 1)

            def ring_slot(t):
                return pe.value_load(TROW[0:1, bass.ds(t * FIELDS + 2, 1)], min_val=0, max_val=RING - 1)

            def gate_up(slot, u):
                for c in range(DC):
                    last = nc.tensor.matmul(bank(2 + u % 2, 0, 2 * F), XT[u % SLOTS][:, c * P:(c + 1) * P],
                                            w_ring[:, bass.ds(slot, 1), c * 2 * F:(c + 1) * 2 * F].squeeze(1),
                                            start=(c == 0), stop=(c == DC - 1))
                last.then_inc(e_GU, 1)

            def hidden_rows_t(t, u):
                pe.wait_ge(e_H, t + 1)
                nc.tensor.transpose(bank(4 + u % 2, 0, P), HH[u % 2], ident[:]).then_inc(e_HP, 1)

            for t in range(4):
                if t >= 2:
                    pe.wait_ge(e_XT, t - 1)
                transposes_of(t, t % 2, 16)
            for t in range(2):
                slot = ring_slot(t)
                pe.wait_ge(e_XT, t + 1)
                gate_up(slot, t)
            hidden_rows_t(0, 0)
            with pe.Fori(0, TILES // LOADED) as n:
                ahead = ring_slot(n * LOADED + 2)
                for u in range(LOADED):
                    t = n * LOADED + u
                    gate_up(ahead, u + 2)
                    slot = ring_slot(t)
                    if u + 1 < LOADED:
                        ahead = ring_slot(t + 3)
                    hidden_rows_t(t + 1, u + 1)
                    transposes_of((u + 4) % LOADED, u % 2, n * 16 + 16 * ((u + 4) // LOADED + 1))
                    pe.wait_ge(e_HT, t + 1)
                    pe.wait_ge(e_O, t + 1)
                    nc.tensor.matmul(bank(6 + u % 2, 0, D), HT[u % 2], w_ring[:, bass.ds(slot, 1), 4 * F:4 * F + D].squeeze(1),
                                     start=True, stop=True).then_inc(e_D, 1)


NAMES = ['x', 'ctx_1024', 'L0_attn_Wq', 'L0_attn_bq', 'L0_attn_Wkv', 'L0_attn_bkv', 'L0_attn_Wo',
         'L0_xattn_norm_w', 'L0_xattn_norm_b', 'L0_xattn_norm1_w', 'L0_xattn_norm1_b', 'L0_xattn_Wq',
         'L0_xattn_bq', 'L0_xattn_Wk', 'L0_xattn_bk', 'L0_xattn_Wv', 'L0_xattn_bv', 'L0_xattn_Wo',
         'L0_xattn_bo', 'L0_ffn_w_router', 'L0_ffn_b_router', 'L0_ffn_we_gate', 'L0_ffn_we_up',
         'L0_ffn_we_down', 'L0_ffn_ws_gate', 'L0_ffn_ws_up', 'L0_ffn_ws_down']


def kernel(**inputs):
    import numpy as np
    import concourse.bacc as bacc
    from concourse.bass_utils import run_bass_kernel_spmd

    nc = bacc.Bacc("TRN2", target_bir_lowering=False, num_devices=1)
    arrays = {n: np.ascontiguousarray(inputs[n]) for n in NAMES}
    freq = np.exp(np.float32(-np.log(10000.0)) * np.arange(0, HD, 2, dtype=np.float32) / np.float32(HD))
    angle = np.arange(T, dtype=np.float32)[None, :] * freq.astype(np.float32)[:, None]
    table = np.empty((HD, T), np.float32)
    table[0::2] = np.sin(angle)
    table[1::2] = np.cos(angle)
    arrays["position_t"] = table
    aps = {n: nc.dram_tensor("in_" + n, v.shape, F32, kind="ExternalInput").ap() for n, v in arrays.items()}
    out = nc.dram_tensor("out", (B, T, D), F32, kind="ExternalOutput").ap()
    build(nc, aps, out)
    r = run_bass_kernel_spmd(nc, [{"in_" + n: v for n, v in arrays.items()}], core_ids=[0])
    return r.results[0]["out"]
```
